# Optimizing a Trainium2 kernel written in Bass

```python
import numpy as np
import jax
import jax.numpy as jnp

def _softmax(x, axis=-1):
    return jax.nn.softmax(x, axis=axis)

def _gelu(x):
    return jax.nn.gelu(x, approximate=True)

def _silu(x):
    return jax.nn.silu(x)

def _sigmoid(x):
    return jax.nn.sigmoid(x)

def _layernorm(x, axis=-1, eps=1e-05):
    m = jnp.mean(x, axis=axis, keepdims=True)
    v = jnp.var(x, axis=axis, keepdims=True)
    return (x - m) / jnp.sqrt(v + eps)

def _scatter_add(tgt, idx, src, axis=0):
    return tgt.at[idx].add(src)

def _segment_sum(src, seg, n):
    return jax.ops.segment_sum(src, seg, n)
kernel_name = 'mk_decoder_postln_d1_seqx_r8_4e7def'

def setup_inputs(seed: int=0):
    np.random.seed(seed)
    _w = jnp.asarray

    def _rec_inputs():
        import jax
        import jax.numpy as jnp
        _rk = jax.random.key(seed)
        x = -0.0002928 + 1 * jax.random.normal(jax.random.fold_in(_rk, 1), (128, 64, 128), jnp.float32)
        _lenS = 64 - jax.random.randint(jax.random.fold_in(_rk, 7), (128,), 0, max(1, 64 // 4) + 1, jnp.int32)
        _lenS2 = 64 - jax.random.randint(jax.random.fold_in(_rk, 8), (128,), 0, max(1, 64 // 4) + 1, jnp.int32)
        _ctx_1024P = jax.random.normal(jax.random.fold_in(_rk, 11), (128, 16, 128), jnp.float32)
        _ctx_1024c = jax.random.dirichlet(jax.random.fold_in(_rk, 511), 0.3 * jnp.ones((16,), jnp.float32), (128, 64))
        _ctx_1024t = jnp.einsum('bsk,bkd->bsd', _ctx_1024c, _ctx_1024P)
        _ctx_1024t = _ctx_1024t * jax.lax.rsqrt(jnp.mean(jnp.square(_ctx_1024t)) + 1e-12) * 0.953939
        ctx_1024 = -1.39393e-06 + 0.999914 * (_ctx_1024t + 0.3 * jax.random.normal(jax.random.fold_in(_rk, 611), (128, 64, 128), jnp.float32))
        return (x, ctx_1024)
    x, ctx_1024 = _rec_inputs()

    def _L0_attn_setup():
        import jax, jax.numpy as jnp
        import numpy as np
        import math
        D_MODEL = 128
        N_HEADS = 16
        D_HEAD = D_MODEL // N_HEADS
        DECAY_MAX = 0.99
        LN_EPS = 1e-05

        def _decay_mask(S):
            i = jnp.arange(S, dtype=jnp.float32)[:, None]
            j = jnp.arange(S, dtype=jnp.float32)[None, :]
            diff = i - j
            return jnp.where(diff >= 0, jnp.power(jnp.float32(DECAY_MAX), diff), 0.0)
        key = jax.random.key(seed)
        ks = jax.random.split(key, 12)
        B, S = (2, 256)
        x = jax.random.normal(ks[0], (B, S, D_MODEL), dtype=jnp.float32)

        def w(k):
            return jax.random.normal(k, (D_MODEL, D_MODEL), dtype=jnp.float32) * 0.02
        return {'x': x, 'Wq': w(ks[1]), 'bq': jnp.zeros((D_MODEL,), jnp.float32), 'Wk': w(ks[2]), 'bk': jnp.zeros((D_MODEL,), jnp.float32), 'Wv': w(ks[3]), 'bv': jnp.zeros((D_MODEL,), jnp.float32), 'Wg': w(ks[4]), 'bg': jnp.zeros((D_MODEL,), jnp.float32), 'Wo': w(ks[5]), 'bo': jnp.zeros((D_MODEL,), jnp.float32), 'gamma': jnp.ones((D_MODEL,), jnp.float32), 'beta': jnp.zeros((D_MODEL,), jnp.float32)}
    _L0_attn_all = _L0_attn_setup()
    _L0_attn_in = {k: v for k, v in _L0_attn_all.items() if k in ('Wq', 'bq', 'Wk', 'bk', 'Wv', 'bv', 'Wg', 'bg', 'Wo', 'bo', 'gamma', 'beta')}
    del _L0_attn_all

    def _L0_xattn_setup():
        import jax, jax.numpy as jnp
        import numpy as np
        B, T, D, H = (2, 256, 128, 16)
        DH = D // H
        key = jax.random.key(seed)
        ks = jax.random.split(key, 11)
        s = 1.0 / np.sqrt(D)
        return {'q': jax.random.normal(ks[0], (B, T, D), jnp.float32), 'k': jax.random.normal(ks[1], (B, T, D), jnp.float32), 'v': jax.random.normal(ks[2], (B, T, D), jnp.float32), 'wq_w': jax.random.normal(ks[3], (D, D), jnp.float32) * s, 'wq_b': jnp.zeros((D,), jnp.float32), 'wk_w': jax.random.normal(ks[4], (D, D), jnp.float32) * s, 'wk_b': jnp.zeros((D,), jnp.float32), 'wv_w': jax.random.normal(ks[5], (D, D), jnp.float32) * s, 'wv_b': jnp.zeros((D,), jnp.float32), 'wo_w': jax.random.normal(ks[6], (D, D), jnp.float32) * s, 'wo_b': jnp.zeros((D,), jnp.float32)}
    _L0_xattn_all = _L0_xattn_setup()
    _L0_xattn_in = {k: v for k, v in _L0_xattn_all.items() if k in ('wq_w', 'wq_b', 'wk_w', 'wk_b', 'wv_w', 'wv_b', 'wo_w', 'wo_b')}
    del _L0_xattn_all

    def _L0_ffn_setup():
        import jax, jax.numpy as jnp
        import numpy as np
        B, S, D, H, E, K, F = (1, 128, 128, 16, 8, 2, 512)

        def layernorm(x, g, b, eps=1e-05):
            m = x.mean(-1, keepdims=True)
            v = ((x - m) ** 2).mean(-1, keepdims=True)
            return (x - m) * jax.lax.rsqrt(v + eps) * g + b
        key = jax.random.key(seed)
        ks = jax.random.split(key, 8)
        n = lambda k, shape, sc: jax.random.normal(k, shape, dtype=jnp.float32) * sc
        return {'x': n(ks[0], (B, S, D), 1.0), 'w_qkv': n(ks[1], (D, 3 * D), D ** (-0.5)), 'w_o': n(ks[2], (D, D), D ** (-0.5)), 'g1': jnp.ones((D,), jnp.float32), 'b1': jnp.zeros((D,), jnp.float32), 'wg': n(ks[3], (D, E), D ** (-0.5)), 'w1': n(ks[4], (E, D, F), D ** (-0.5)), 'bb1': jnp.zeros((E, F), jnp.float32), 'w2': n(ks[5], (E, F, D), F ** (-0.5)), 'bb2': jnp.zeros((E, D), jnp.float32), 'g2': jnp.ones((D,), jnp.float32), 'b2': jnp.zeros((D,), jnp.float32)}
    _L0_ffn_all = _L0_ffn_setup()
    _L0_ffn_in = {k: v for k, v in _L0_ffn_all.items() if k in ('w_qkv', 'w_o', 'g1', 'b1', 'wg', 'w1', 'bb1', 'w2', 'bb2', 'g2', 'b2')}
    del _L0_ffn_all
    return {'x': x, 'ctx_1024': ctx_1024, 'L0_attn_Wq': _L0_attn_in['Wq'], 'L0_attn_bq': _L0_attn_in['bq'], 'L0_attn_Wk': _L0_attn_in['Wk'], 'L0_attn_bk': _L0_attn_in['bk'], 'L0_attn_Wv': _L0_attn_in['Wv'], 'L0_attn_bv': _L0_attn_in['bv'], 'L0_attn_Wg': _L0_attn_in['Wg'], 'L0_attn_bg': _L0_attn_in['bg'], 'L0_attn_Wo': _L0_attn_in['Wo'], 'L0_attn_bo': _L0_attn_in['bo'], 'L0_attn_gamma': _L0_attn_in['gamma'], 'L0_attn_beta': _L0_attn_in['beta'], 'L0_xattn_wq_w': _L0_xattn_in['wq_w'], 'L0_xattn_wq_b': _L0_xattn_in['wq_b'], 'L0_xattn_wk_w': _L0_xattn_in['wk_w'], 'L0_xattn_wk_b': _L0_xattn_in['wk_b'], 'L0_xattn_wv_w': _L0_xattn_in['wv_w'], 'L0_xattn_wv_b': _L0_xattn_in['wv_b'], 'L0_xattn_wo_w': _L0_xattn_in['wo_w'], 'L0_xattn_wo_b': _L0_xattn_in['wo_b'], 'L0_ffn_w_qkv': _L0_ffn_in['w_qkv'], 'L0_ffn_w_o': _L0_ffn_in['w_o'], 'L0_ffn_g1': _L0_ffn_in['g1'], 'L0_ffn_b1': _L0_ffn_in['b1'], 'L0_ffn_wg': _L0_ffn_in['wg'], 'L0_ffn_w1': _L0_ffn_in['w1'], 'L0_ffn_bb1': _L0_ffn_in['bb1'], 'L0_ffn_w2': _L0_ffn_in['w2'], 'L0_ffn_bb2': _L0_ffn_in['bb2'], 'L0_ffn_g2': _L0_ffn_in['g2'], 'L0_ffn_b2': _L0_ffn_in['b2']}

def reference(x, ctx_1024, L0_attn_Wq, L0_attn_bq, L0_attn_Wk, L0_attn_bk, L0_attn_Wv, L0_attn_bv, L0_attn_Wg, L0_attn_bg, L0_attn_Wo, L0_attn_bo, L0_attn_gamma, L0_attn_beta, L0_xattn_wq_w, L0_xattn_wq_b, L0_xattn_wk_w, L0_xattn_wk_b, L0_xattn_wv_w, L0_xattn_wv_b, L0_xattn_wo_w, L0_xattn_wo_b, L0_ffn_w_qkv, L0_ffn_w_o, L0_ffn_g1, L0_ffn_b1, L0_ffn_wg, L0_ffn_w1, L0_ffn_bb1, L0_ffn_w2, L0_ffn_bb2, L0_ffn_g2, L0_ffn_b2):
    import jax
    import jax.numpy as jnp

    def _L0_attn_ref(x, Wq, bq, Wk, bk, Wv, bv, Wg, bg, Wo, bo, gamma, beta):
        import jax, jax.numpy as jnp
        import numpy as np
        import math
        D_MODEL = 128
        N_HEADS = 16
        D_HEAD = D_MODEL // N_HEADS
        DECAY_MAX = 0.99
        LN_EPS = 1e-05

        def _decay_mask(S):
            i = jnp.arange(S, dtype=jnp.float32)[:, None]
            j = jnp.arange(S, dtype=jnp.float32)[None, :]
            diff = i - j
            return jnp.where(diff >= 0, jnp.power(jnp.float32(DECAY_MAX), diff), 0.0)
        B, S, D = x.shape
        H, DH = (N_HEADS, D_HEAD)
        Q = (x @ Wq + bq).reshape(B, S, H, DH).transpose(0, 2, 1, 3)
        K = (x @ Wk + bk).reshape(B, S, H, DH).transpose(0, 2, 1, 3)
        V = (x @ Wv + bv).reshape(B, S, H, DH).transpose(0, 2, 1, 3)
        scores = jnp.einsum('bhsd,bhtd->bhst', Q, K) / math.sqrt(DH)
        mask = _decay_mask(S)
        retained = jnp.einsum('bhst,bhtd->bhsd', scores * mask, V)
        retained = retained.transpose(0, 2, 1, 3).reshape(B, S, D)
        mu = jnp.mean(retained, axis=-1, keepdims=True)
        var = jnp.var(retained, axis=-1, keepdims=True)
        normed = (retained - mu) * jax.lax.rsqrt(var + LN_EPS) * gamma + beta
        G = jax.nn.sigmoid(x @ Wg + bg)
        return normed * G @ Wo + bo

    def _L0_xattn_ref(q, k, v, wq_w, wq_b, wk_w, wk_b, wv_w, wv_b, wo_w, wo_b):
        import jax, jax.numpy as jnp
        import numpy as np
        B, T, D, H = (2, 256, 128, 16)
        DH = D // H
        b, t, d = q.shape
        wq = (q @ wq_w.T + wq_b).reshape(b, t, H, DH)
        wk = (k @ wk_w.T + wk_b).reshape(b, t, H, DH)
        wv = (v @ wv_w.T + wv_b).reshape(b, t, H, DH)
        scores = jnp.einsum('bthd,bshd->bhts', wq, wk) / jnp.sqrt(jnp.float32(DH))
        probs = jax.nn.softmax(scores, axis=-1)
        attn = jnp.einsum('bhts,bshd->bthd', probs, wv)
        attn = attn.reshape(b, t, d)
        return attn @ wo_w.T + wo_b

    def _L0_ffn_ref(x, w_qkv, w_o, g1, b1, wg, w1, bb1, w2, bb2, g2, b2):
        import jax, jax.numpy as jnp
        import numpy as np
        B, S, D, H, E, K, F = (1, 128, 128, 16, 8, 2, 512)

        def layernorm(x, g, b, eps=1e-05):
            m = x.mean(-1, keepdims=True)
            v = ((x - m) ** 2).mean(-1, keepdims=True)
            return (x - m) * jax.lax.rsqrt(v + eps) * g + b
        b, s, d = x.shape
        hd = d // H
        qkv = x @ w_qkv
        q, k, v = jnp.split(qkv, 3, axis=-1)
        to_heads = lambda t: t.reshape(b, s, H, hd).transpose(0, 2, 1, 3)
        q, k, v = (to_heads(q), to_heads(k), to_heads(v))
        scores = jnp.einsum('bhqd,bhkd->bhqk', q, k) / jnp.sqrt(jnp.float32(hd))
        causal = jnp.tril(jnp.ones((s, s), bool))
        scores = jnp.where(causal, scores, jnp.finfo(scores.dtype).min)
        attn = jax.nn.softmax(scores, axis=-1)
        o = jnp.einsum('bhqk,bhkd->bhqd', attn, v)
        o = o.transpose(0, 2, 1, 3).reshape(b, s, d) @ w_o
        h = layernorm(x + o, g1, b1)
        probs = jax.nn.softmax(h @ wg, axis=-1)
        topv, topi = jax.lax.top_k(probs, K)
        topv = topv / topv.sum(-1, keepdims=True)
        w = (topv[..., None] * jax.nn.one_hot(topi, E, dtype=h.dtype)).sum(-2)
        h1 = jax.nn.gelu(jnp.einsum('bsd,edf->ebsf', h, w1) + bb1[:, None, None, :])
        y = jnp.einsum('ebsf,efd->ebsd', h1, w2) + bb2[:, None, None, :]
        moe = jnp.einsum('ebsd,bse->bsd', y, w)
        return layernorm(h + moe, g2, b2)
    x = _layernorm(x + _L0_attn_ref(x, L0_attn_Wq, L0_attn_bq, L0_attn_Wk, L0_attn_bk, L0_attn_Wv, L0_attn_bv, L0_attn_Wg, L0_attn_bg, L0_attn_Wo, L0_attn_bo, L0_attn_gamma, L0_attn_beta), axis=-1)
    x = _layernorm(x + _L0_xattn_ref(x, ctx_1024, ctx_1024, L0_xattn_wq_w, L0_xattn_wq_b, L0_xattn_wk_w, L0_xattn_wk_b, L0_xattn_wv_w, L0_xattn_wv_b, L0_xattn_wo_w, L0_xattn_wo_b), axis=-1)
    x = _layernorm(x + _L0_ffn_ref(x, L0_ffn_w_qkv, L0_ffn_w_o, L0_ffn_g1, L0_ffn_b1, L0_ffn_wg, L0_ffn_w1, L0_ffn_bb1, L0_ffn_w2, L0_ffn_bb2, L0_ffn_g2, L0_ffn_b2), axis=-1)
    return x

_drawn_inputs = setup_inputs


def setup_inputs(seed=0):
    import zlib

    import numpy as np

    out = dict(_drawn_inputs(seed))
    spreads = {'L0_attn_bq': (0.0, 0.1),
     'L0_attn_bk': (0.0, 0.1),
     'L0_attn_bv': (0.0, 0.1),
     'L0_attn_bg': (0.0, 0.595),
     'L0_attn_bo': (0.0, 0.1),
     'L0_attn_gamma': (1.0, 0.2),
     'L0_attn_beta': (0.0, 0.339),
     'L0_xattn_wq_b': (0.0, 0.1),
     'L0_xattn_wk_b': (0.0, 0.8),
     'L0_xattn_wv_b': (0.0, 0.1),
     'L0_xattn_wo_b': (0.0, 0.1),
     'L0_ffn_g1': (1.0, 0.2),
     'L0_ffn_b1': (0.0, 0.1),
     'L0_ffn_bb1': (0.0, 0.34),
     'L0_ffn_bb2': (0.0, 0.1),
     'L0_ffn_g2': (1.0, 0.2),
     'L0_ffn_b2': (0.0, 0.1)}
    factors = {'L0_attn_Wg': 2.773}
    for name, (base, spread) in spreads.items():
        noise = np.random.default_rng([zlib.crc32(name.encode()), seed]).standard_normal(out[name].shape)
        drawn = base * np.exp(spread * noise) if base else spread * noise
        out[name] = jnp.asarray(drawn.astype(out[name].dtype))
    for name, factor in factors.items():
        out[name] = (out[name] * factor).astype(out[name].dtype)
    return out
```

```python
from contextlib import ExitStack

import numpy as np
import concourse.bass as bass
from concourse import mybir

F32 = mybir.dt.float32
F16 = mybir.dt.float16
BF16 = mybir.dt.bfloat16
U32 = mybir.dt.uint32
ALU = mybir.AluOpType
ACT = mybir.ActivationFunctionType
AX_X = mybir.AxisListType.X

P = 128
S = 64
H = 16
DH = 8
NG = 4
PAIRS = H // 2
TPG = 2
GT = TPG * P
TPB = 8
GPB = TPB // TPG
EPS = 1e-5
SCALE = DH ** -0.5
MAX_ROW = 24
E_N = 8
F_N = 512
FC = F_N // P

COLS = ["a_bq", "a_bk", "a_bg", "a_gamma", "a_beta", "x_bq", "x_bk", "x_bv", "ones_row", "k_zero"]
ROWS = ["a_bv", "a_bo", "x_bo", "g1", "b1", "g2", "b2"]


def head_of(g, i):
    return (i % 2) * 8 + 2 * g + i // 2


def shape_constants():
    ident = np.eye(P, dtype=np.float32)
    sel = np.zeros((P, 4, NG, P), np.float32)
    for g in range(NG):
        for i in range(4):
            for d in range(DH):
                src, row = head_of(g, i) * DH + d, 32 * i + d
                sel[src, 0, g, row] = sel[src, 0, g, row + 8] = sel[src, 1, g, row + 16] = 1
                sel[src, 2, g, row] = sel[src, 2, g, row + 16] = sel[src, 3, g, row + 8] = 1
    s = np.arange(P) % S
    diff = np.arange(S)[None, :] - s[:, None]
    decay = np.where(diff >= 0, np.power(np.float32(0.99), diff.astype(np.float32)), 0).astype(np.float32)
    decay = (decay * np.float32(SCALE)).astype(np.float32)
    mask_t = np.where(diff >= 0, 0, -1e30).astype(np.float32)
    mask_s = np.where(diff <= 0, 0, -1e30).astype(np.float32)
    ones_row = np.zeros(P, np.float32)
    ones_row[MAX_ROW::32] = 1
    return ident, sel.reshape(P, -1), np.concatenate([decay, mask_t, mask_s], 1), ones_row


class Event:

    def __init__(self, ctx, nc, name, per_body, inc=1, turns=2):
        self.sems = [ctx.enter_context(nc.semaphore(f"{name}{r}")) for r in range(turns)]
        self.turns, self.rounds, self.inc, self.base = turns, per_body // turns, inc, 0

    def at(self, idx):
        m, k = idx
        return self.sems[k % self.turns], m * self.rounds + k // self.turns

    def mark(self, instruction, idx):
        instruction.then_inc(self.at(idx)[0], self.inc)
        return instruction

    def wait(self, engine, idx):
        sem, m = self.at(idx)
        if isinstance(m, int) and m < 0:
            return
        engine.wait_ge(sem, (m + (self.base + 1)) * self.inc)


def build(nc, x, ctxt, wmats, cols, rows, const_ident, const_sel, const_masks, const_eid, wg, w1, bb1t, w2, bb2, out, upto=4):
    T_N = x.shape[0] * x.shape[1]
    NT = T_N // P
    NQ = NT // TPG
    NB = NT // TPB
    pe, dve, act, pool, sp = nc.tensor, nc.vector, nc.scalar, nc.gpsimd, nc.sync
    ctx = ExitStack()

    def sb(name, shape, dt=F32):
        return ctx.enter_context(nc.sbuf_tensor(name, shape, dt))

    def event(name, per_body, inc=1, turns=2):
        e = Event(ctx, nc, name, per_body, inc, turns)
        events.append(e)
        return e

    events = []
    ident = sb("ident", [P, P])
    ident16 = sb("ident16", [P, P], F16)
    ident_b = sb("ident_b", [P, P], BF16)
    sel_f = sb("sel_f", [P, 4 * NG * P])
    sel = sb("sel", [P, 4, NG, P], F16)
    masks_f = sb("masks_f", [P, 3 * S])
    masks_b = sb("masks_b", [P, 2, S], BF16)
    decay = masks_f[:, 0:S]
    W = sb("W", [P, wmats.shape[0], P])
    col = sb("col", [P, len(COLS)])
    row = sb("row", [P, len(ROWS), P])
    wg_sb = sb("wg_sb", [P, E_N])

    xg = [sb(f"xg{p}", [P, TPG, P]) for p in range(4)]
    cg = [sb(f"cg{p}", [P, TPG, P]) for p in range(2)]
    xb = [sb(f"xb{p}", [P, TPG, P]) for p in range(4)]
    srcT = [sb(f"srcT{p}", [P, 2, GT]) for p in range(2)]
    hilo = [sb(f"hilo{p}", [P, 4, GT], F16) for p in range(2)]
    Qst = [sb(f"Qst{p}", [P, NG, GT], F16) for p in range(2)]
    Kst = [sb(f"Kst{p}", [P, NG, GT], F16) for p in range(2)]
    V32 = [sb(f"V32_{p}", [P, TPG, P]) for p in range(2)]
    Vh = [sb(f"Vh{p}", [P, TPG, PAIRS, 2 * DH + 1], F16) for p in range(4)]
    Vl = [sb(f"Vl{p}", [P, TPG, PAIRS, 2 * DH], F16) for p in range(4)]
    GTs = [sb(f"GTs{p}", [P, GT]) for p in range(4)]
    mx = [sb(f"mx{t}", [P, NG, P], F16) for t in range(2)]
    Qm = [sb(f"Qm{t}", [P, NG, P], F16) for t in range(2)]
    P32 = [sb(f"P32_{t}", [P, H, S]) for t in range(2)]
    Plo = [sb(f"Plo{t}", [P, H, S], F16) for t in range(2)]
    rden = [sb(f"rden{t}", [P, 2, PAIRS]) for t in range(2)]
    O = [sb(f"O{p}", [P, TPG, P]) for p in range(2)]
    On = [sb(f"On{p}", [P, TPG, P]) for p in range(2)]
    OT = [sb(f"OT{p}", [P, GT]) for p in range(2)]
    OTg = [sb(f"OTg{p}", [P, GT]) for p in range(2)]
    r = [sb(f"r{p}", [P, TPG, P]) for p in range(2)]
    y = [sb(f"y{p}", [P, TPG, P]) for p in range(2)]
    st = [sb(f"st{p}", [P, TPG, 6]) for p in range(2)]
    mv = [sb(f"mv{p}", [P, TPG, 2]) for p in range(2)]
    ve = [sb(f"ve{p}", [P, TPG]) for p in range(2)]
    rstd = [sb(f"rstd{p}", [P, TPG]) for p in range(2)]
    hn = [sb(f"hn{p}", [P, TPG, P]) for p in range(2)]
    hg = [sb(f"hg{p}", [P, TPG, P]) for p in range(2)]
    junk = sb("junk", [P, 1])
    minus_half = sb("minus_half", [P, TPG])

    bank = ctx.enter_context(nc.psum_tensor("bank", [P, 8, 512], F32))
    S_BANK, T_BANK, PV_BANK, MA, MB = 0, 2, 4, 6, 7
    bankA, bankB = bank[:, MA, :], bank[:, MB, :]

    x1 = nc.dram_tensor("x1_scratch", (T_N, P), F32).ap()
    x2 = nc.dram_tensor("x2_scratch", (T_N, P), F32).ap()
    hd = nc.dram_tensor("h_scratch", (T_N, P), F32).ap()

    ld = event("ld", GPB, 16, 4)
    ldc = event("ldc", GPB, 16)
    sto = event("sto", GPB, 16)
    e_xT = event("xT", GPB)
    e_xTs = event("xTs", GPB)
    e_QK = event("QK", GPB)
    e_hi = event("hi", GPB)
    e_lo = event("lo", GPB)
    e_V = event("V", GPB)
    e_V32 = event("V32", GPB)
    e_Vh = event("Vh", GPB)
    e_Vl = event("Vl", GPB)
    e_gate = event("gate", GPB)
    e_sel = [event(f"sel{j}", GPB) for j in range(2)]
    e_Qs = [event(f"Qs{j}", GPB) for j in range(2)]
    e_Ks = [event(f"Ks{j}", GPB) for j in range(2)]
    e_S = event("S", TPB)
    e_Si = [event(f"Si{i}", TPB) for i in range(2)]
    e_Ti = [event(f"Ti{i}", TPB) for i in range(2)]
    e_mx = event("mx", TPB)
    e_mT = event("mT", TPB)
    e_Qm = event("Qm", TPB)
    e_T = event("T", TPB)
    e_P = event("P", TPB)
    e_Pl = event("Pl", TPB)
    e_PV = event("PV", TPB)
    e_rd = event("rd", TPB)
    e_O = event("O", TPB)
    e_xb = event("xb", GPB)
    e_st = event("st", GPB)
    e_mv = event("mv", GPB)
    e_ve = event("ve", GPB)
    e_rs = event("rs", GPB)
    e_On = event("On", GPB)
    f_st, f_mv, f_ve, f_rs = (event(n, GPB) for n in ("fst", "fmv", "fve", "frs"))
    e_OT = event("OT", GPB)
    e_OTs = event("OTs", GPB)
    e_OTg = event("OTg", GPB)
    e_out = event("out", GPB)
    e_r = event("r", GPB)
    e_y = event("y", GPB)
    e_hn = event("hn", GPB)
    e_hg = event("hg", GPB)
    s_ld = ctx.enter_context(nc.semaphore("s_ld"))
    s_set = ctx.enter_context(nc.semaphore("s_set"))
    s_bar = ctx.enter_context(nc.semaphore("s_bar"))
    barriers = [0]

    def carrier():
        dve.memset(junk[:, :], 0.0)

    def barrier():
        barriers[0] += 1
        for e in (pe, dve, act, pool, sp):
            e.drain().then_inc(s_bar, 1)
        for e in (pe, dve, act, pool, sp):
            e.wait_ge(s_bar, 5 * barriers[0])

    loads = 0
    for dst, src in ((ident[:, :], const_ident), (sel_f[:, :], const_sel), (masks_f[:, :], const_masks),
                     (W[:, :, :], wmats.rearrange("w p n -> p w n")), (col[:, :], cols),
                     (wg_sb[:, :], wg)):
        sp.dma_start(dst, src).then_inc(s_ld, 16)
        loads += 16
    for n in range(len(ROWS)):
        sp.dma_start(row[:, n, :], rows[n:n + 1, :].broadcast_to([P, P])).then_inc(s_ld, 16)
        loads += 16
    for t in range(2):
        pool.memset(mx[t][:, :, :], 0.0).then_inc(s_set, 1)
    for t in range(4):
        pool.memset(Vh[t][:, :, :, :], 1.0).then_inc(s_set, 1)
    for e in (sto, e_OT, e_OTg, e_out, e_y):
        for sem in e.sems:
            pool.sem_inc(sem, e.inc)
        e.base = 1
    pool.memset(minus_half[:, :], -0.5).then_inc(s_set, 1)
    dve.wait_ge(s_ld, loads)
    dve.tensor_copy(ident16[:, :], ident[:, :]).then_inc(s_set, 1)
    dve.tensor_copy(ident_b[:, :], ident[:, :]).then_inc(s_set, 1)
    dve.tensor_copy(sel[:, :, :, :].rearrange("p a g n -> p (a g n)"), sel_f[:, :]).then_inc(s_set, 1)
    dve.tensor_copy(masks_b[:, :, :].rearrange("p a n -> p (a n)"), masks_f[:, S:]).then_inc(s_set, 1)
    for e in (pe, act, pool, dve):
        e.wait_ge(s_ld, loads)
        e.wait_ge(s_set, 11)

    def column(name):
        k = COLS.index(name)
        return col[:, k:k + 1]

    def brow(name):
        return row[:, ROWS.index(name), :].unsqueeze(1).broadcast_to([P, TPG, P])

    def attention_phase(kind, src, dst, unused):
        ret, cross, causal = kind == "ret", kind == "cross", kind == "self"
        w0 = {"ret": 0, "cross": 5, "self": 9}[kind]
        WQ, WK, WV, WO = (W[:, w0 + j, :] for j in range(4))
        bq = {"ret": "a_bq", "cross": "x_bq", "self": "k_zero"}[kind]
        bk = {"ret": "a_bk", "cross": "x_bk", "self": "k_zero"}[kind]
        src_g = src.rearrange("(q t p) d -> q p t d", t=TPG, p=P)
        dst_g = dst.rearrange("(q t p) d -> q p t d", t=TPG, p=P)
        ctx_g = ctxt.rearrange("(q t p) d -> q p t d", t=TPG, p=P)
        kv = 1 if cross else 0

        def dram(ap, idx):
            m, k = idx
            q = m * GPB + k
            return ap[q] if isinstance(q, int) else ap[bass.ds(q, 1)].rearrange("o p t d -> (o p) t d")

        def load(q):
            p = q[1] % 2
            y_before = (q[0], q[1] - 2)
            if causal:
                e_r.wait(sp, (q[0], q[1] - 4))
            else:
                e_xb.wait(sp, (q[0], q[1] - 4))
                e_xT.wait(sp, (q[0], q[1] - 4))
            ld.mark(sp.dma_start(xg[q[1] % 4][:, :, :], dram(src_g, q)), q)
            if cross:
                e_xT.wait(sp, y_before)
                ldc.mark(sp.dma_start(cg[p][:, :, :], dram(ctx_g, q)), q)

        def turn_inputs(q):
            p = q[1] % 2
            e_Ks[1].wait(pe, (q[0], q[1] - 1))
            ld.wait(pe, q)
            for t in range(TPG):
                i = pe.transpose(bankA[:, t * P:(t + 1) * P], xg[q[1] % 4][:, t, :], ident[:, :])
            if cross:
                ldc.wait(pe, q)
                for t in range(TPG):
                    i = pe.transpose(bankA[:, GT + t * P:GT + (t + 1) * P], cg[p][:, t, :], ident[:, :])
            e_xT.mark(i, q)
            e_V.wait(act, (q[0], q[1] - 2))
            e_xT.wait(act, q)
            n = 1 + kv
            e_xTs.mark(act.copy(srcT[p][:, 0:n, :].rearrange("p a t -> p (a t)"), bankA[:, 0:n * GT]), q)
            if not causal:
                e_r.wait(pool, (q[0], q[1] - 4))
                ld.wait(pool, q)
                e_xb.mark(pool.tensor_tensor(xb[q[1] % 4][:, :, :], xg[q[1] % 4][:, :, :],
                                               brow("a_bo" if ret else "x_bo"), ALU.add), q)

        def project_qk(q):
            p = q[1] % 2
            e_Qs[1].wait(pe, (q[0], q[1] - 1))
            e_xTs.wait(pe, q)
            pe.matmul(bankB[:, 0:GT], WQ, srcT[p][:, 0, :], start=True, stop=True)
            e_QK.mark(pe.matmul(bankB[:, GT:2 * GT], WK, srcT[p][:, kv, :], start=True, stop=True), q)
            e_sel[1].wait(act, (q[0], q[1] - 2))
            e_QK.wait(act, q)
            act.activation(hilo[p][:, 0, :], bankB[:, 0:GT], ACT.Identity, bias=column(bq))
            e_hi.mark(act.activation(hilo[p][:, 2, :], bankB[:, GT:2 * GT], ACT.Identity, bias=column(bk)), q)
            e_hi.wait(dve, q)
            dve.scalar_tensor_tensor(out=hilo[p][:, 1, :], in0=bankB[:, 0:GT], scalar=column(bq),
                                     in1=hilo[p][:, 0, :], op0=ALU.add, op1=ALU.subtract)
            e_lo.mark(dve.scalar_tensor_tensor(out=hilo[p][:, 3, :], in0=bankB[:, GT:2 * GT], scalar=column(bk),
                                                 in1=hilo[p][:, 2, :], op0=ALU.add, op1=ALU.subtract), q)

        def project_v(q, free_a):
            p = q[1] % 2
            free_a(pe)
            for t in range(TPG):
                i = pe.matmul(bankA[:, t * P:(t + 1) * P], srcT[p][:, kv, t * P:(t + 1) * P], WV,
                              start=True, stop=True)
            if ret:
                i = pe.matmul(bankA[:, GT:2 * GT], W[:, w0 + 4, :], srcT[p][:, 0, :], start=True, stop=True)
            e_V.mark(i, q)

            def parts(v):
                return v.rearrange("p t (j e) -> p t j e", e=2 * DH)

            tiles_before = (q[0], TPG * (q[1] - 4) + TPG - 1)
            e_PV.wait(act, tiles_before)
            vh = Vh[q[1] % 4][:, :, :, 0:2 * DH]
            vp = bankA[:, 0:GT].rearrange("p (t j e) -> p t j e", t=TPG, e=2 * DH)
            if ret:
                e_V.wait(dve, q)
                e_V32.mark(dve.tensor_tensor(V32[p][:, :, :], bankA[:, 0:GT].rearrange("p (t d) -> p t d", t=TPG),
                                               brow("a_bv"), ALU.add), q)
                e_V32.wait(act, q)
                vp = V32[p][:, :, :].rearrange("p t (j e) -> p t j e", e=2 * DH)
                e_OTg.wait(act, (q[0], q[1] - 4))
                e_gate.mark(act.activation(GTs[q[1] % 4][:, :], bankA[:, GT:2 * GT], ACT.Sigmoid, bias=column("a_bg")), q)
            e_V.wait(act, q)
            for t in range(TPG):
                i = act.copy(vh[:, t], vp[:, t])
            e_Vh.mark(i, q)
            e_Vh.wait(dve, q)
            for t in range(TPG):
                i = dve.tensor_tensor(Vl[q[1] % 4][:, t], vp[:, t], vh[:, t], ALU.subtract)
            e_Vl.mark(i, q)

        def stack(q, j, free_a, free_b):
            p = q[1] % 2
            e_lo.wait(pe, q)
            free_b(pe)
            for g in (2 * j, 2 * j + 1):
                o = bankB[:, (g % 2) * GT:(g % 2 + 1) * GT]
                pe.matmul(o, sel[:, 0, g, :], hilo[p][:, 0, :], start=True, stop=False)
                pe.matmul(o, sel[:, 1, g, :], hilo[p][:, 1, :], start=False, stop=True)
            free_a(pe)
            for g in (2 * j, 2 * j + 1):
                o = bankA[:, (g % 2) * GT:(g % 2 + 1) * GT]
                pe.matmul(o, sel[:, 2, g, :], hilo[p][:, 2, :], start=True, stop=False)
                i = pe.matmul(o, sel[:, 3, g, :], hilo[p][:, 3, :], start=False, stop=True)
            e_sel[j].mark(i, q)
            tiles_before = (q[0], TPG * (q[1] - 2) + TPG - 1)
            for e in (act, dve):
                e_T.wait(e, tiles_before)
            e_sel[j].wait(act, q)
            e_Qs[j].mark(act.copy(Qst[p][:, 2 * j:2 * j + 2, :].rearrange("p g t -> p (g t)"), bankB[:, :]), q)
            e_sel[j].wait(dve, q)
            e_Ks[j].mark(dve.tensor_scalar(Kst[p][:, 2 * j:2 * j + 2, :].rearrange("p g t -> p (g t)"), bankA[:, :],
                                             column("ones_row"), None, ALU.add), q)

        def group_of(n):
            return (n[0], n[1] // TPG)

        def score_tile(n, strips, banks, left, left_at, right, right_at, mask):
            if mask is not None:
                for h in range(2):
                    pe.matmul(bank[:, banks + h, :].rearrange("p (k s) -> p k s", k=8), ident_b[:, :],
                              mask.unsqueeze(1).broadcast_to([P, 8, S]), start=True, stop=False, skip_group_check=True)
            for i in range(4):
                if i >= 2:
                    strips[i - 2].wait(pe, n)
                for g in range(NG):
                    slot = 2 * g + i // 2
                    for b in range(2):
                        inst = pe.matmul(bank[64 * b:64 * b + 64, banks + i % 2, slot * S:(slot + 1) * S],
                                         left[32 * i:32 * i + 32, g, left_at + b * S:left_at + (b + 1) * S],
                                         right[32 * i:32 * i + 32, g, right_at + b * S:right_at + (b + 1) * S],
                                         start=mask is None, stop=True, skip_group_check=mask is not None)
                if i < 2:
                    strips[i].mark(inst, n)
            return inst

        def scores_s(n):
            q, p, t = group_of(n), group_of(n)[1] % 2, n[1] % 2
            if t == 0:
                e_Qs[1].wait(pe, q)
                e_Ks[1].wait(pe, q)
            e_mx.wait(pe, (n[0], n[1] - 1))
            at = (n[1] % TPG) * P
            e_S.mark(score_tile(n, e_Si, S_BANK, Qst[p], at, Kst[p], at, masks_b[:, 1, :] if causal else None), n)

        def maxima(n):
            e_S.wait(dve, n)
            e_mT.wait(dve, (n[0], n[1] - 2))
            t = n[1] % 2
            full = mx[t][:, :, :].rearrange("p g (k h c) -> p h (g k) c", k=2, h=2, c=32)[:, :, :, MAX_ROW]
            e_mx.mark(dve.tensor_reduce(full, bank[:, S_BANK:S_BANK + 2, :].rearrange("p h (k s) -> p h k s", s=S),
                                          AX_X, ALU.max, negate=True), n)

        def turn_maxima(n, free_a):
            t = n[1] % 2
            free_a(pe)
            e_mx.wait(pe, n)
            for g in range(NG):
                i = pe.matmul(bankA[:, g * P:(g + 1) * P], mx[t][:, g, :], ident16[:, :], start=True, stop=True)
            e_mT.mark(i, n)
            q = group_of(n)
            at = (n[1] % TPG) * P
            e_T.wait(dve, (n[0], n[1] - 2))
            e_mT.wait(dve, n)
            e_Qm.mark(dve.tensor_tensor(Qm[t][:, :, :], bankA[:, :].rearrange("p (g s) -> p g s", g=NG),
                                          Qst[q[1] % 2][:, :, at:at + P], ALU.add), n)

        def scores_t(n):
            q, p, t = group_of(n), group_of(n)[1] % 2, n[1] % 2
            at = (n[1] % TPG) * P
            tb = (S_BANK if t else T_BANK) if ret else T_BANK
            if ret:
                if t == 0:
                    e_Qs[1].wait(pe, q)
                    e_Ks[1].wait(pe, q)
                e_P.wait(pe, (n[0], n[1] - 2))
                right, right_at = Qst[p], at
            else:
                e_Qm.wait(pe, n)
                e_P.wait(pe, (n[0], n[1] - 1))
                right, right_at = Qm[t], 0
            e_T.mark(score_tile(n, e_Ti, tb, Kst[p], at, right, right_at, masks_b[:, 0, :] if causal else None), n)
            e = dve if ret else act
            e_T.wait(e, n)
            e_PV.wait(e, (n[0], n[1] - 2))
            e_Pl.wait(e, (n[0], n[1] - 2))
            sc = bank[:, tb:tb + 2, :].rearrange("p h (k s) -> p (h k) s", s=S)
            if ret:
                e_P.mark(dve.tensor_tensor(P32[t][:, :, :], sc, decay.unsqueeze(1).broadcast_to([P, H, S]),
                                             ALU.mult), n)
            else:
                e_P.mark(act.activation(P32[t][:, :, :], sc, ACT.Exp, scale=SCALE), n)

        def upper(t):
            return P32[t][:, :, :].rearrange("p k s -> p (k s)").bitcast(BF16)[:, 1::2]

        def weights_lo(n):
            t = n[1] % 2
            e_P.wait(pool, n)
            e_PV.wait(pool, (n[0], n[1] - 2))
            e_Pl.mark(pool.tensor_tensor(Plo[t][:, :, :].rearrange("p k s -> p (k s)"),
                                           P32[t][:, :, :].rearrange("p k s -> p (k s)"), upper(t), ALU.subtract), n)

        def weighted_sums(n):
            q, p, t, tt = group_of(n), group_of(n)[1] % 2, n[1] % 2, n[1] % TPG
            nv = 2 * DH if ret else 2 * DH + 1
            e_Vl.wait(pe, q)
            e_O.wait(pe, (n[0], n[1] - 1))
            e_P.wait(pe, n)
            e_Pl.wait(pe, n)
            up = upper(t)
            lo = Plo[t][:, :, :].rearrange("p k s -> p (k s)")
            for b in range(2):
                rows_b = slice(64 * b, 64 * b + 64)
                for j in range(PAIRS):
                    c = slice(j * P, (j + 1) * P)
                    o = bank[:, PV_BANK + b, j * 32:j * 32 + nv]
                    pe.matmul(o, up[rows_b, c], Vh[q[1] % 4][rows_b, tt, j, 0:nv], start=True, stop=False)
                    pe.matmul(o, lo[rows_b, c], Vh[q[1] % 4][rows_b, tt, j, 0:nv], start=False, stop=False)
                    i = pe.matmul(o[:, 0:2 * DH], up[rows_b, c], Vl[q[1] % 4][rows_b, tt, j, :], start=False, stop=True)
            e_PV.mark(i, n)
            pv = bank[:, PV_BANK:PV_BANK + 2, 0:PAIRS * 32].rearrange("p b (j c) -> p b j c", c=32)
            e_OT.wait(dve, (q[0], q[1] - 2)) if not ret else e_On.wait(dve, (q[0], q[1] - 2))
            e_PV.wait(dve, n)
            if not ret:
                e_rd.mark(dve.reciprocal(rden[t][:, :, :], pv[:, :, :, 2 * DH]), n)
                e_rd.wait(dve, n)
            ov = O[p][:, tt, :].rearrange("p (j i e) -> p j i e", i=2, e=DH)
            for b in range(2):
                for i2 in range(2):
                    rs_ = slice(64 * i2, 64 * i2 + 64)
                    o = ov[64 * b:64 * b + 64, :, i2, :]
                    a = pv[rs_, b, :, i2 * DH:(i2 + 1) * DH]
                    if ret:
                        i = dve.tensor_copy(o, a)
                    else:
                        i = dve.tensor_tensor(o, a, rden[t][rs_, b, :].unsqueeze(2).broadcast_to([64, PAIRS, DH]),
                                              ALU.mult)
            e_O.mark(i, n)

        def norm_scalars(q, v, evs, ready):
            p = q[1] % 2
            s1, s2, s3, s4 = evs
            ready(dve)
            for t in range(TPG):
                i = dve.bn_stats(st[p][:, t, :], v[:, t, :])
            s1.mark(i, q)
            s1.wait(dve, q)
            carrier()
            for t in range(TPG):
                i = dve.bn_aggr(mv[p][:, t, :], st[p][:, t, :])
            s2.mark(i, q)
            s2.wait(dve, q)
            s3.mark(dve.tensor_scalar(ve[p][:, :], mv[p][:, :, 1], EPS, None, ALU.add), q)
            s3.wait(pool, q)
            s4.mark(pool.tensor_tensor(rstd[p][:, :], ve[p][:, :], minus_half[:, :], ALU.pow), q)
            s4.wait(dve, q)

        def normalise(q, o, v, ev):
            p = q[1] % 2
            for t in range(TPG):
                i = dve.tensor_scalar(o[:, t, :], v[:, t, :], mv[p][:, t, 0:1], rstd[p][:, t:t + 1],
                                      ALU.subtract, ALU.mult)
            ev.mark(i, q)

        def norm_retained(q):
            last = (q[0], TPG * q[1] + TPG - 1)
            norm_scalars(q, O[q[1] % 2], (e_st, e_mv, e_ve, e_rs), lambda e: e_O.wait(e, last))
            e_OT.wait(dve, (q[0], q[1] - 2))
            normalise(q, On[q[1] % 2], O[q[1] % 2], e_On)

        def turn_result(q, free_b):
            p = q[1] % 2
            free_b(pe)
            if ret:
                e_On.wait(pe, q)
                v = On[p]
            else:
                e_O.wait(pe, (q[0], TPG * q[1] + TPG - 1))
                v = O[p]
            for t in range(TPG):
                i = pe.transpose(bankB[:, t * P:(t + 1) * P], v[:, t, :], ident[:, :])
            e_OT.mark(i, q)
            before = (q[0], q[1] - 2)
            if ret:
                e_OTg.wait(dve, before)
                e_OT.wait(dve, q)
                e_OTs.mark(dve.tensor_scalar(OT[p][:, :], bankB[:, 0:GT], column("a_gamma"), column("a_beta"),
                                               ALU.mult, ALU.add), q)
                e_OTs.wait(dve, q)
                e_gate.wait(dve, q)
                e_out.wait(dve, before)
                e_OTg.mark(dve.tensor_tensor(OTg[p][:, :], OT[p][:, :], GTs[q[1] % 4][:, :], ALU.mult), q)
            else:
                e_out.wait(act, before)
                e_OT.wait(act, q)
                e_OTs.mark(act.activation(OT[p][:, :], bankB[:, 0:GT], ACT.Identity,
                                            bias=column("x_bv" if cross else "k_zero")), q)

        def project_out(q):
            p = q[1] % 2
            src_t = OTg[p] if ret else OT[p]
            (e_OTg if ret else e_OTs).wait(pe, q)
            for t in range(TPG):
                i = pe.matmul(bankB[:, t * P:(t + 1) * P], src_t[:, t * P:(t + 1) * P], WO, start=True, stop=True)
            e_out.mark(i, q)
            e_out.wait(dve, q)
            if not causal:
                e_xb.wait(dve, q)
            e_y.wait(dve, (q[0], q[1] - 2))
            e_r.mark(dve.tensor_tensor(r[p][:, :, :], bankB[:, 0:GT].rearrange("p (t d) -> p t d", t=TPG),
                                         (xg if causal else xb)[q[1] % 4][:, :, :], ALU.add), q)

        def finish(q):
            p = q[1] % 2
            norm_scalars(q, r[p], (f_st, f_mv, f_ve, f_rs), lambda e: e_r.wait(e, q))
            sto.wait(dve, (q[0], q[1] - 2))
            if not causal:
                normalise(q, y[p], r[p], e_y)
                return
            e_hn.wait(dve, (q[0], q[1] - 2))
            normalise(q, hn[p], r[p], e_hn)
            e_hn.wait(pool, q)
            e_hg.mark(pool.tensor_tensor(hg[p][:, :, :], hn[p][:, :, :], brow("g1"), ALU.mult), q)
            e_hg.wait(pool, q)
            sto.wait(pool, (q[0], q[1] - 2))
            e_y.mark(pool.tensor_tensor(y[p][:, :, :], hg[p][:, :, :], brow("b1"), ALU.add), q)

        def store(q):
            e_y.wait(act, q)
            sto.mark(act.dma_start(dram(dst_g, q), y[q[1] % 2][:, :, :]), q)

        def step(m, k, steps):

            def tile(lag):
                s = None if steps is None else steps - lag
                return (m, k - lag), s is None or 0 <= s < NT

            def group(lag):
                s = None if steps is None else (steps - lag) // TPG
                return (m, (k - lag) // TPG), s is None or 0 <= s < NQ

            even = k % 2 == 0
            q, on_q = group(k % 2)
            n2, on2 = tile(2)
            n3, on3 = tile(3)
            n4, on4 = tile(4)
            q4, on_q4 = group(8)
            q3, on_q3 = group(6 + k % 2)
            if even and on_q:
                load(q)
            if even and on_q4:
                store(q4)
            if not ret and on3:
                scores_t(n3)
            if ret and on2:
                scores_t(n2)
            if not ret and on2:
                scores_s(n2)
                maxima(n2)
            if on4:
                weighted_sums(n4)
            if even:
                if on_q:
                    turn_inputs(q)
                    project_qk(q)
                if not ret and on2:
                    def free_a(e):
                        e_Ks[1].wait(e, (q[0], q[1] - 1))
                        if on_q:
                            e_xTs.wait(e, q)
                    turn_maxima(n2, free_a)
                if on_q:
                    def free_a(e):
                        e_xTs.wait(e, q)
                        if not ret and on2:
                            e_Qm.wait(e, n2)
                    project_v(q, free_a)
                if on_q3:
                    if ret:
                        norm_retained(q3)

                    def free_b(e):
                        if on_q:
                            e_hi.wait(e, q)
                            e_lo.wait(e, q)
                        e_r.wait(e, (q3[0], q3[1] - 1))
                    turn_result(q3, free_b)
                    project_out(q3)
            else:
                if on_q:
                    def free_b(e):
                        e_lo.wait(e, q)
                        if on_q3:
                            e_r.wait(e, q3)

                    def free_a(e):
                        e_Vl.wait(e, q)
                        e_Vh.wait(e, q)
                        if ret:
                            e_gate.wait(e, q)
                    stack(q, 0, free_a, free_b)
                if not ret and on2:
                    def free_a(e):
                        if on_q:
                            e_Ks[0].wait(e, q)
                        else:
                            e_Qm.wait(e, (n2[0], n2[1] - 1))
                    turn_maxima(n2, free_a)
                if on_q:
                    def free_a(e):
                        e_Ks[0].wait(e, q)
                        if not ret and on2:
                            e_Qm.wait(e, n2)
                    stack(q, 1, free_a, lambda e: e_Qs[0].wait(e, q))
                if on_q3:
                    finish(q3)
            if ret and on2:
                weights_lo(n2)
            if not ret and on3:
                weights_lo(n3)

        for k in range(TPB):
            step(0, k, k)
        with nc.Fori(1, NB) as m:
            for k in range(TPB):
                step(m, k, None)
        for k in range(TPB):
            step(NB, k, NB * TPB + k)
        for k in (GPB - 2, GPB - 1):
            sto.wait(sp, (NB - 1, k))
        barrier()
        for e in events:
            if e not in unused:
                e.base += NB * e.rounds


    MT = 4
    NS = NT // MT
    w1_sb = sb("w1_sb", [P, E_N, F_N])
    w2_sb = sb("w2_sb", [P, E_N, FC, P])
    b1_sb = sb("b1_sb", [P, E_N * FC])
    b2_sb = sb("b2_sb", [E_N, P])
    eid = sb("eid", [P, E_N])
    s_w = ctx.enter_context(nc.semaphore("s_w"))
    sp.dma_start(w1_sb[:, :, :], w1.rearrange("e d f -> d e f")).then_inc(s_w, 16)
    sp.dma_start(w2_sb[:, :, :, :], w2.rearrange("e (c f) d -> f e c d", f=P)).then_inc(s_w, 16)
    sp.dma_start(b1_sb[:, :], bb1t).then_inc(s_w, 16)
    sp.dma_start(b2_sb[:, :], bb2).then_inc(s_w, 16)
    sp.dma_start(eid[:, :], const_eid.broadcast_to([P, E_N])).then_inc(s_w, 16)

    h_t = [sb(f"h_t{p}", [P, MT, P]) for p in range(2)]
    x_t = [sb(f"x_t{p}", [P, MT, P]) for p in range(2)]
    hT = sb("hT", [P, MT * P])
    lg = sb("lg", [P, MT, E_N])
    top = sb("top", [P, MT, 8])
    topi = sb("topi", [P, MT, 8], U32)
    topf = sb("topf", [P, MT, 8])
    d12 = sb("d12", [P, MT])
    e12 = sb("e12", [P, MT])
    s12 = sb("s12", [P, MT])
    wa = sb("wa", [P, MT])
    wb = sb("wb", [P, MT])
    ma = sb("ma", [P, MT, E_N])
    mb_ = sb("mb_", [P, MT, E_N])
    wt = sb("wt", [P, MT, E_N])
    wT = sb("wT", [E_N, MT, P])
    G = [sb(f"G{p}", [P, FC, MT * P]) for p in range(2)]
    acc = sb("acc", [P, MT, P])
    t1 = sb("t1", [P, MT, P])
    t2 = sb("t2", [P, MT, P])
    res = [sb(f"res{p}", [P, MT, P]) for p in range(2)]
    mst = sb("mst", [P, MT, 6])
    mmv = sb("mmv", [P, MT, 2])
    mve = sb("mve", [P, MT])
    mrs = sb("mrs", [P, MT])
    mh4 = sb("mh4", [P, MT])

    def moe_phase(h_src, x_src, dst):
        hg_, xg_, og_ = (a.rearrange("(q t p) d -> q p t d", t=MT, p=P) for a in (h_src, x_src, dst))
        ev = {n: [ctx.enter_context(nc.semaphore("m_" + n)), 0, per] for n, per in (
            ("hT", 1), ("hTs", 1), ("lg", 1), ("lgs", 1), ("dv", 16 + 0), ("ex", 1), ("w", 1), ("wT", 1), ("wTs", 1),
            ("bb", 1), ("acc0", 1), ("z", E_N * FC), ("g", E_N * FC), ("y", E_N), ("acc", E_N), ("ps", 2), ("fin", 1))}
        mld = [ctx.enter_context(nc.semaphore(f"m_ld{p}")) for p in range(2)]
        mst_ = [ctx.enter_context(nc.semaphore(f"m_st{p}")) for p in range(2)]

        def sig(name, inst, at, last=False):
            inst.then_inc(ev[name][0], 1)
            ev[name][1] += 1
            return (name, ev[name][1])

        def wait(e, name, m, k):
            v = m * ev[name][2] + k
            if isinstance(v, int) and v <= 0:
                return
            e.wait_ge(ev[name][0], v)

        pool.memset(mh4[:, :], -0.5).then_inc(s_set, 1)
        for e in (pe, dve, act, pool):
            e.wait_ge(s_w, 16 * 5)
            e.wait_ge(s_set, 12)

        def body(u, half, s):
            p = half
            n = [0]

            def dchain(inst):
                n[0] += 1
                inst.then_inc(ev["dv"][0], 1)
                wait(dve, "dv", s, n[0])
                carrier()

            wait(sp, "fin", s, -1)
            src = (lambda a: a[s] if isinstance(s, int) else a[bass.ds(s, 1)].rearrange("o p t d -> (o p) t d"))
            sp.dma_start(h_t[p][:, :, :], src(hg_)).then_inc(mld[p], 16)
            sp.dma_start(x_t[p][:, :, :], src(xg_)).then_inc(mld[p], 16)
            pe.wait_ge(mld[p], (u + 1) * 32)
            wait(pe, "acc", s, 0)
            for t in range(MT):
                i = pe.transpose(bank[:, 0, t * P:(t + 1) * P], h_t[p][:, t, :], ident[:, :])
            sig("hT", i, s)
            wait(act, "hT", s, 1)
            wait(act, "z", s, 0)
            sig("hTs", act.copy(hT[:, :], bank[:, 0, :]), s)
            wait(pe, "hTs", s, 1)
            for t in range(MT):
                i = pe.matmul(bank[:, 1, t * E_N:(t + 1) * E_N], hT[:, t * P:(t + 1) * P], wg_sb[:, :], start=True, stop=True)
            sig("lg", i, s)
            wait(dve, "lg", s, 1)
            dchain(dve.tensor_copy(lg[:, :, :].rearrange("p t e -> p (t e)"), bank[:, 1, 0:MT * E_N]))
            for t in range(MT):
                i = dve.max(top[:, t, :], lg[:, t, :])
            dchain(i)
            for t in range(MT):
                i = dve.max_index(topi[:, t, :], top[:, t, :], lg[:, t, :])
            dchain(i)
            dchain(dve.tensor_copy(topf[:, :, :], topi[:, :, :]))
            i = dve.tensor_tensor(d12[:, :], top[:, :, 1], top[:, :, 0], ALU.subtract)
            dchain(i)
            wait(act, "dv", s, n[0])
            sig("ex", act.activation(e12[:, :], d12[:, :], ACT.Exp), s)
            wait(dve, "ex", s, 1)
            dchain(dve.tensor_scalar(s12[:, :], e12[:, :], 1.0, None, ALU.add))
            dchain(dve.reciprocal(wa[:, :], s12[:, :]))
            dchain(dve.tensor_tensor(wb[:, :], wa[:, :], e12[:, :], ALU.mult))
            eb = eid[:, :].unsqueeze(1).broadcast_to([P, MT, E_N])
            dchain(dve.tensor_tensor(ma[:, :, :], eb, topf[:, :, 0:1].broadcast_to([P, MT, E_N]), ALU.is_equal))
            dchain(dve.tensor_tensor(mb_[:, :, :], eb, topf[:, :, 1:2].broadcast_to([P, MT, E_N]), ALU.is_equal))
            dchain(dve.tensor_tensor(ma[:, :, :], ma[:, :, :], wa[:, :].unsqueeze(2).broadcast_to([P, MT, E_N]), ALU.mult))
            dchain(dve.tensor_tensor(mb_[:, :, :], mb_[:, :, :], wb[:, :].unsqueeze(2).broadcast_to([P, MT, E_N]), ALU.mult))
            sig("w", dve.tensor_tensor(wt[:, :, :], ma[:, :, :], mb_[:, :, :], ALU.add), s)
            wait(dve, "w", s, 1)
            wait(pe, "w", s, 1)
            for t in range(MT):
                i = pe.transpose(bank[0:E_N, 1, t * P:(t + 1) * P], wt[:, t, :], ident[:, :])
            sig("wT", i, s)
            wait(act, "wT", s, 1)
            sig("wTs", act.copy(wT[:, :, :].rearrange("p t n -> p (t n)"), bank[0:E_N, 1, :]), s)
            wait(pe, "wTs", s, 1)
            for t in range(MT):
                i = pe.matmul(bank[:, 1, t * P:(t + 1) * P], wT[:, t, :], b2_sb[:, :], start=True, stop=True)
            sig("bb", i, s)
            wait(dve, "bb", s, 1)
            sig("acc0", dve.tensor_tensor(acc[:, :, :], bank[:, 1, :].rearrange("p (t d) -> p t d", t=MT), h_t[p][:, :, :], ALU.add), s)
            wait(dve, "acc0", s, 1)

            def up(e):
                for c in range(FC):
                    j = e * FC + c
                    wait(pe, "g", s, j - 2 + 1)
                    if j == 0:
                        wait(pe, "hTs", s, 1)
                    zb = 2 + j % 2
                    sig("z", pe.matmul(bank[:, zb, :], w1_sb[:, e, c * P:(c + 1) * P], hT[:, :], start=True, stop=True), s)
                    wait(act, "z", s, j + 1)
                    if c == 0:
                        wait(act, "y", s, e - 1)
                    sig("g", act.activation(G[e % 2][:, c, :], bank[:, zb, :], ACT.Gelu_apprx_tanh, bias=b1_sb[:, j:j + 1]), s)

            def down(e):
                wait(pe, "g", s, (e + 1) * FC)
                wait(pe, "acc", s, e - 1)
                yb = 4 + e % 2
                for t in range(MT):
                    for c in range(FC):
                        i = pe.matmul(bank[:, yb, t * P:(t + 1) * P], G[e % 2][:, c, t * P:(t + 1) * P], w2_sb[:, e, c, :],
                                      start=c == 0, stop=c == FC - 1)
                sig("y", i, s)
                wait(dve, "y", s, e + 1)
                if e:
                    wait(dve, "acc", s, e)
                for t in range(MT):
                    i = dve.scalar_tensor_tensor(out=acc[:, t, :], in0=bank[:, yb, t * P:(t + 1) * P], scalar=wt[:, t, e:e + 1],
                                                 in1=acc[:, t, :], op0=ALU.mult, op1=ALU.add)
                sig("acc", i, s)

            up(0)
            for e in range(E_N):
                if e + 1 < E_N:
                    up(e + 1)
                down(e)
            wait(dve, "acc", s, E_N)

            def norm(o, v, k):
                for t in range(MT):
                    i = dve.bn_stats(mst[:, t, :], v[:, t, :])
                dchain(i)
                for t in range(MT):
                    i = dve.bn_aggr(mmv[:, t, :], mst[:, t, :])
                dchain(i)
                dchain(dve.tensor_scalar(mve[:, :], mmv[:, :, 1], EPS, None, ALU.add))
                wait(pool, "dv", s, n[0])
                sig("ps", pool.tensor_tensor(mrs[:, :], mve[:, :], mh4[:, :], ALU.pow), s)
                wait(dve, "ps", s, k)
                for t in range(MT):
                    i = dve.tensor_scalar(o[:, t, :], v[:, t, :], mmv[:, t, 0:1], mrs[:, t:t + 1], ALU.subtract, ALU.mult)
                return i

            def br(name):
                return row[:, ROWS.index(name), :].unsqueeze(1).broadcast_to([P, MT, P])

            dchain(norm(t1, acc, 1))
            dchain(dve.tensor_tensor(t2[:, :, :], t1[:, :, :], br("g2"), ALU.mult))
            dchain(dve.tensor_tensor(t1[:, :, :], t2[:, :, :], br("b2"), ALU.add))
            dchain(dve.tensor_tensor(t2[:, :, :], t1[:, :, :], x_t[p][:, :, :], ALU.add))
            if not (isinstance(u, int) and u == 0):
                dve.wait_ge(mst_[p], u * 16)
            sig("fin", norm(res[p], t2, 2), s)
            wait(act, "fin", s, 1)
            act.dma_start(src(og_), res[p][:, :, :]).then_inc(mst_[p], 16)
            ev["dv"][2] = n[0]

        ev["dv"][2] = 22
        for half in range(2):
            body(0, half, half)
        with nc.Fori(1, NS // 2) as u:
            for half in range(2):
                body(u, half, u * 2 + half)
        assert ev["dv"][2] == 22, ev["dv"][2]
        for p in range(2):
            sp.wait_ge(mst_[p], 16 * (NS // 2))

    xf = x.rearrange("b s d -> (b s) d")
    ctxt = ctxt.rearrange("b s d -> (b s) d")
    outf = out.rearrange("b s d -> (b s) d")
    targets = [x1, x2, hd]
    softmax_only = [e_S, *e_Si, e_mx, e_mT, e_Qm, e_rd]
    self_only = [e_hn, e_hg]
    retention_only = [e_V32, e_gate, e_OTg, e_st, e_mv, e_ve, e_rs, e_On]
    attention_phase("ret", xf, outf if upto == 1 else x1, [ldc, *softmax_only, *self_only])
    if upto >= 2:
        attention_phase("cross", x1, outf if upto == 2 else x2, [*retention_only, *self_only])
    if upto >= 3:
        attention_phase("self", x2, outf if upto == 3 else hd, [ldc, e_xb, *retention_only])
    if upto >= 4:
        moe_phase(hd, x2, outf)
    return ctx, events


def lay_out(inputs):
    a = {k: np.asarray(v) for k, v in inputs.items()}
    A, X, N = (lambda n: a["L0_attn_" + n]), (lambda n: a["L0_xattn_" + n]), (lambda n: a["L0_ffn_" + n])
    ident, sel, masks, ones_row = shape_constants()
    qkv = N("w_qkv")
    wmats = np.stack([A("Wq"), A("Wk"), A("Wv"), A("Wo"), A("Wg"),
                      X("wq_w").T, X("wk_w").T, X("wv_w").T, X("wo_w").T,
                      qkv[:, 0:P], qkv[:, P:2 * P], qkv[:, 2 * P:], N("w_o")])
    cols = np.stack([A("bq"), A("bk"), A("bg"), A("gamma"), A("beta"), X("wq_b"), X("wk_b"), X("wv_b"),
                     ones_row, np.zeros(P, np.float32)], 1)
    rows = np.stack([A("bv"), A("bo"), X("wo_b"), N("g1"), N("b1"), N("g2"), N("b2")])
    c = np.ascontiguousarray
    return {"x": a["x"], "ctxt": a["ctx_1024"], "wmats": c(wmats), "cols": c(cols), "rows": c(rows),
            "const_ident": ident, "const_sel": sel, "const_masks": masks, "const_eid": np.arange(E_N, dtype=np.float32)[None], "wg": N("wg"),
            "w1": N("w1"), "bb1t": c(N("bb1").reshape(E_N * FC, P).T), "w2": N("w2"), "bb2": N("bb2")}


def kernel(**inputs):
    import concourse.bacc as _bacc
    from concourse.bass_utils import run_bass_kernel_spmd as _run

    nc = _bacc.Bacc("TRN2", target_bir_lowering=False, num_devices=1)
    arrays = lay_out(inputs)
    args = {n: nc.dram_tensor(n, a.shape, mybir.dt.from_np(a.dtype), kind="ExternalInput").ap()
            for n, a in arrays.items()}
    out = nc.dram_tensor("out", arrays["x"].shape, F32, kind="ExternalOutput").ap()
    build(nc, **args, out=out)
    r = _run(nc, [arrays], core_ids=[0])
    return r.results[0]["out"]
```

```python
from contextlib import ExitStack

import numpy as np
import concourse.bass as bass
from concourse import mybir

F32 = mybir.dt.float32
F16 = mybir.dt.float16
BF16 = mybir.dt.bfloat16
U32 = mybir.dt.uint32
ALU = mybir.AluOpType
ACT = mybir.ActivationFunctionType
AX_X = mybir.AxisListType.X

P = 128
S = 64
H = 16
DH = 8
NG = 4
PAIRS = H // 2
TPG = 2
GT = TPG * P
TPB = 8
GPB = TPB // TPG
EPS = 1e-5
SCALE = DH ** -0.5
MAX_ROW = 24
E_N = 8
F_N = 512
FC = F_N // P

COLS = ["a_bq", "a_bk", "a_bg", "a_gamma", "a_beta", "x_bq", "x_bk", "x_bv", "ones_row", "k_zero"]
ROWS = ["a_bv", "a_bo", "x_bo", "g1", "b1", "g2", "b2"]


def head_of(g, i):
    return (i % 2) * 8 + 2 * g + i // 2


def shape_constants():
    ident = np.eye(P, dtype=np.float32)
    sel = np.zeros((P, 4, NG, P), np.float32)
    for g in range(NG):
        for i in range(4):
            for d in range(DH):
                src, row = head_of(g, i) * DH + d, 32 * i + d
                sel[src, 0, g, row] = sel[src, 0, g, row + 8] = sel[src, 1, g, row + 16] = 1
                sel[src, 2, g, row] = sel[src, 2, g, row + 16] = sel[src, 3, g, row + 8] = 1
    s = np.arange(P) % S
    diff = np.arange(S)[None, :] - s[:, None]
    decay = np.where(diff >= 0, np.power(np.float32(0.99), diff.astype(np.float32)), 0).astype(np.float32)
    decay = (decay * np.float32(SCALE)).astype(np.float32)
    mask_t = np.where(diff >= 0, 0, -1e30).astype(np.float32)
    mask_s = np.where(diff <= 0, 0, -1e30).astype(np.float32)
    ones_row = np.zeros(P, np.float32)
    ones_row[MAX_ROW::32] = 1
    return ident, sel.reshape(P, -1), np.concatenate([decay, mask_t, mask_s], 1), ones_row


def routing_constants(tiles):
    f, n = np.float32, tiles * P
    p = np.arange(P)[:, None]
    ids = 2 * P + np.arange(2)[None, :, None] * n + np.arange(tiles)[None, None] * P + p[:, :, None]
    return {"const_ids": ids.reshape(P, -1).astype(f), "const_tri": np.triu(np.ones((P, P), f), 1),
            "const_rev": (E_N - np.arange(E_N, dtype=f))[None], "const_steps": np.arange(tiles, dtype=f)[None] * P,
            "const_blocks": np.arange(2 * tiles + E_N, dtype=f)[None],
            "const_trash": (p + P * np.arange(2)[None]).astype(f)}


class Event:

    def __init__(self, sems, per_body, inc, origin=0):
        self.sems, self.turns, self.inc, self.origin = sems, len(sems), inc, origin
        self.rounds = per_body // self.turns

    def at(self, idx):
        m, k = idx
        return self.sems[k % self.turns], m * self.rounds + k // self.turns

    def mark(self, instruction, idx):
        instruction.then_inc(self.at(idx)[0], self.inc)
        return instruction

    def wait(self, engine, idx):
        sem, m = self.at(idx)
        k = idx[1]
        if isinstance(m, int) and m < 0:
            return
        assert isinstance(m, int) or self.rounds + k // self.turns + self.origin // self.inc + 1 > 0, (self.sems[0].name, idx)
        engine.wait_ge(sem, m * self.inc + (self.inc + self.origin))

    def happened(self, bodies):
        self.origin += bodies * self.rounds * self.inc


def build(nc, x, ctxt, wmats, cols, rows, const_ident, const_sel, const_masks, const_ids, const_tri, const_rev, const_steps, const_blocks, const_trash, wg, w1, bb1t, w2, bb2, out, upto=4):
    T_N = x.shape[0] * x.shape[1]
    NT = T_N // P
    NQ = NT // TPG
    NB = NT // TPB
    pe, dve, act, pool, sp = nc.tensor, nc.vector, nc.scalar, nc.gpsimd, nc.sync
    ctx = ExitStack()
    in_ctx = [ctx]

    def sb(name, shape, dt=F32):
        return in_ctx[-1].enter_context(nc.sbuf_tensor(name, shape, dt))

    def event(name, per_body, inc=1, turns=2, fresh=False):
        for old in free:
            if not fresh and (old.inc > 1) == (inc > 1) and old.turns == turns:
                free.remove(old)
                e = Event(old.sems, per_body, inc, old.origin)
                break
        else:
            e = Event([ctx.enter_context(nc.semaphore(f"{name}{r}")) for r in range(turns)], per_body, inc)
        events.append(e)
        return e

    free = []
    events = []
    ident = sb("ident", [P, P])
    ident16 = sb("ident16", [P, P], F16)
    ident_b = sb("ident_b", [P, P], BF16)
    sel_f = sb("sel_f", [P, 4 * NG * P])
    sel = sb("sel", [P, 4, NG, P], F16)
    masks_f = sb("masks_f", [P, 3 * S])
    masks_b = sb("masks_b", [P, 2, S], BF16)
    decay = masks_f[:, 0:S]
    W = sb("W", [P, wmats.shape[0], P])
    col = sb("col", [P, len(COLS)])
    row = sb("row", [P, len(ROWS), P])
    wg_sb = sb("wg_sb", [P, E_N])

    MT = 4
    NS = NT // MT
    U = 2 * NT
    NBLK = U + E_N
    BPB = 4
    EPB = 8
    RW = P + 1
    WW = 2 * F_N + FC + P
    W1, W2, B1, B2 = 0, F_N, 2 * F_N, 2 * F_N + FC
    TRASH = 2 * P
    buf = nc.dram_tensor("block_rows", (NBLK * P, RW), F32).ap()
    ydst = nc.dram_tensor("expert_rows", (TRASH + 2 * T_N, P), F32).ap()

    wx = sb("wx", [P, E_N, WW])
    zeros = sb("zeros", [P, 8 * RW])
    s_w = ctx.enter_context(nc.semaphore("s_w"))
    s_fill = ctx.enter_context(nc.semaphore("s_fill"))
    s_zero = ctx.enter_context(nc.semaphore("s_zero"))
    ids = sb("ids", [P, 2, NT])
    tri = sb("tri", [P, P])
    rev = sb("rev", [P, E_N])
    steps128 = sb("steps128", [P, NT])
    blocks_row = sb("blocks_row", [P, NBLK])
    trash = sb("trash", [P, 2])
    ones = sb("ones", [P, P])

    junk = sb("junk", [P, 256])
    junk_p = sb("junk_p", [P, 64])
    minus_half = sb("minus_half", [P, TPG])

    attention_ctx = ExitStack()
    in_ctx[0] = attention_ctx
    xg = [sb(f"xg{p}", [P, TPG, P]) for p in range(4)]
    cg = [sb(f"cg{p}", [P, TPG, P]) for p in range(2)]
    xb = [sb(f"xb{p}", [P, TPG, P]) for p in range(4)]
    srcT = [sb(f"srcT{p}", [P, 2, GT]) for p in range(2)]
    hilo = [sb(f"hilo{p}", [P, 4, GT], F16) for p in range(2)]
    Qst = [sb(f"Qst{p}", [P, NG, GT], F16) for p in range(2)]
    Kst = [sb(f"Kst{p}", [P, NG, GT], F16) for p in range(2)]
    V32 = [sb(f"V32_{p}", [P, TPG, P]) for p in range(2)]
    Vh = [sb(f"Vh{p}", [P, TPG, PAIRS, 2 * DH + 1], F16) for p in range(4)]
    Vl = [sb(f"Vl{p}", [P, TPG, PAIRS, 2 * DH], F16) for p in range(4)]
    GTs = [sb(f"GTs{p}", [P, GT]) for p in range(4)]
    mx = [sb(f"mx{t}", [P, NG, P], F16) for t in range(2)]
    Qm = [sb(f"Qm{t}", [P, NG, P], F16) for t in range(2)]
    P32 = [sb(f"P32_{t}", [P, H, S]) for t in range(2)]
    Plo = [sb(f"Plo{t}", [P, H, S], F16) for t in range(2)]
    rden = [sb(f"rden{t}", [P, 2, PAIRS]) for t in range(2)]
    O = [sb(f"O{p}", [P, TPG, P]) for p in range(2)]
    On = [sb(f"On{p}", [P, TPG, P]) for p in range(2)]
    OT = [sb(f"OT{p}", [P, GT]) for p in range(2)]
    OTg = [sb(f"OTg{p}", [P, GT]) for p in range(2)]
    r = [sb(f"r{p}", [P, TPG, P]) for p in range(2)]
    y = [sb(f"y{p}", [P, TPG, P]) for p in range(2)]
    st, mv, ve, rstd = ([[sb(f"{n_}{j}{p}", [P, TPG, w_]) for p in range(2)] for j in range(2)]
                        for n_, w_ in (("st", 6), ("mv", 2), ("ve", 1), ("rstd", 1)))
    hn = [sb(f"hn{p}", [P, TPG, P]) for p in range(2)]
    hg = [sb(f"hg{p}", [P, TPG, P]) for p in range(2)]

    in_ctx[0] = ctx

    bank = ctx.enter_context(nc.psum_tensor("bank", [P, 8, 512], F32))
    S_BANK, T_BANK, PV_BANK, MA, MB = 0, 2, 4, 6, 7
    bankA, bankB = bank[:, MA, :], bank[:, MB, :]

    x1 = nc.dram_tensor("x1_scratch", (T_N, P), F32).ap()
    x2 = nc.dram_tensor("x2_scratch", (T_N, P), F32).ap()
    hd = nc.dram_tensor("h_scratch", (T_N, P), F32).ap()

    ld = event("ld", GPB, 16, 4)
    ldc = event("ldc", GPB, 16)
    sto = event("sto", GPB, 16)
    e_xT = event("xT", GPB)
    e_xTs = event("xTs", GPB)
    e_QK = event("QK", GPB)
    e_hi = event("hi", GPB)
    e_lo = event("lo", GPB)
    e_V = event("V", GPB)
    e_V32 = event("V32", GPB)
    e_Vh = event("Vh", GPB)
    e_Vl = event("Vl", GPB)
    e_gate = event("gate", GPB)
    e_sel = [event(f"sel{j}", GPB) for j in range(2)]
    e_Qs = [event(f"Qs{j}", GPB) for j in range(2)]
    e_Ks = [event(f"Ks{j}", GPB) for j in range(2)]
    e_S = event("S", TPB)
    e_Si = [event(f"Si{i}", TPB) for i in range(2)]
    e_Ti = [event(f"Ti{i}", TPB) for i in range(2)]
    e_mx = event("mx", TPB)
    e_mT = event("mT", TPB)
    e_Qm = event("Qm", TPB)
    e_T = event("T", TPB)
    e_P = event("P", TPB)
    e_Pl = event("Pl", TPB)
    e_PV = event("PV", TPB)
    e_rd = event("rd", TPB)
    e_O = event("O", TPB)
    e_xb = event("xb", GPB)
    e_st = event("st", GPB)
    e_mv = event("mv", GPB)
    e_ve = event("ve", GPB)
    e_rs = event("rs", GPB)
    e_On = event("On", GPB)
    f_st, f_mv, f_ve, f_rs = (event(n, GPB) for n in ("fst", "fmv", "fve", "frs"))
    e_OT = event("OT", GPB)
    e_OTs = event("OTs", GPB)
    e_OTg = event("OTg", GPB)
    e_out = event("out", GPB)
    e_r = event("r", GPB)
    e_y = event("y", GPB)
    e_hn = event("hn", GPB)
    e_hg = event("hg", GPB)
    s_ld = ctx.enter_context(nc.semaphore("s_ld"))
    s_set = ctx.enter_context(nc.semaphore("s_set"))
    s_bar = ctx.enter_context(nc.semaphore("s_bar"))
    barriers = [0]

    carriers = [0, 0]

    def carrier():
        carriers[0] += 1
        dve.memset(junk[:, carriers[0]:carriers[0] + 1], 0.0)

    def barrier():
        barriers[0] += 1
        for e in (pe, dve, act, pool, sp):
            e.drain().then_inc(s_bar, 1)
        for e in (pe, dve, act, pool, sp):
            e.wait_ge(s_bar, 5 * barriers[0])

    loads = 0
    for dst, src in ((ident[:, :], const_ident), (sel_f[:, :], const_sel), (masks_f[:, :], const_masks),
                     (W[:, :, :], wmats.rearrange("w p n -> p w n")), (col[:, :], cols),
                     (wg_sb[:, :], wg)):
        sp.dma_start(dst, src).then_inc(s_ld, 16)
        loads += 16
    for n in range(len(ROWS)):
        sp.dma_start(row[:, n, :], rows[n:n + 1, :].broadcast_to([P, P])).then_inc(s_ld, 16)
        loads += 16
    for t in range(2):
        pool.memset(mx[t][:, :, :], 0.0).then_inc(s_set, 1)
    for t in range(4):
        pool.memset(Vh[t][:, :, :, :], 1.0).then_inc(s_set, 1)
    for e in (sto, e_OT, e_OTg, e_out, e_y, e_hn):
        for sem in e.sems:
            pool.sem_inc(sem, e.inc)
        e.origin = e.inc
    pool.memset(minus_half[:, :], -0.5).then_inc(s_set, 1)
    dve.wait_ge(s_ld, loads)
    dve.tensor_copy(ident16[:, :], ident[:, :]).then_inc(s_set, 1)
    dve.tensor_copy(ident_b[:, :], ident[:, :]).then_inc(s_set, 1)
    dve.tensor_copy(sel[:, :, :, :].rearrange("p a g n -> p (a g n)"), sel_f[:, :]).then_inc(s_set, 1)
    dve.tensor_copy(masks_b[:, :, :].rearrange("p a n -> p (a n)"), masks_f[:, S:]).then_inc(s_set, 1)
    for e in (pe, act, pool, dve):
        e.wait_ge(s_ld, loads)
        e.wait_ge(s_set, 11)

    for dst_, src_ in ((wx[:, :, W1:W1 + F_N], w1.rearrange("e d f -> d e f")),
                       (wx[:, :, B1:B1 + FC], bb1t.rearrange("p (e c) -> p e c", c=FC)),
                       (wx[:, :, B2:B2 + P], bb2.rearrange("e d -> (e d)").unsqueeze(0).broadcast_to([P, E_N * P])
                        .rearrange("p (e d) -> p e d", d=P)),
                       (ids[:, :, :].rearrange("p c t -> p (c t)"), const_ids), (tri[:, :], const_tri),
                       (rev[:, :], const_rev.broadcast_to([P, E_N])),
                       (steps128[:, :], const_steps.broadcast_to([P, NT])),
                       (blocks_row[:, :], const_blocks.broadcast_to([P, NBLK])), (trash[:, :], const_trash)):
        sp.dma_start(dst_, src_).then_inc(s_w, 16)
    for e_ in range(E_N):
        sp.dma_start(wx[:, e_, W2:W2 + F_N].rearrange("f (c d) -> f c d", d=P),
                     w2[e_].rearrange("(c f) d -> f c d", f=P)).then_inc(s_w, 16)
    moe_loads = 16 * (9 + E_N)
    pool.memset(zeros[:, :], 0.0).then_inc(s_zero, 1)
    sp.wait_ge(s_zero, 1)
    zero_src = zeros[:, :].unsqueeze(1).broadcast_to([P, NBLK // 8, 8 * RW])
    sp.dma_start(buf.rearrange("(c p j) w -> p c (j w)", p=P, j=8), zero_src).then_inc(s_fill, 16)

    def column(name):
        k = COLS.index(name)
        return col[:, k:k + 1]

    def brow(name):
        return row[:, ROWS.index(name), :].unsqueeze(1).broadcast_to([P, TPG, P])

    def attention_phase(kind, src, dst, unused):
        ret, cross, causal = kind == "ret", kind == "cross", kind == "self"
        w0 = {"ret": 0, "cross": 5, "self": 9}[kind]
        WQ, WK, WV, WO = (W[:, w0 + j, :] for j in range(4))
        bq = {"ret": "a_bq", "cross": "x_bq", "self": "k_zero"}[kind]
        bk = {"ret": "a_bk", "cross": "x_bk", "self": "k_zero"}[kind]
        src_g = src.rearrange("(q t p) d -> q p t d", t=TPG, p=P)
        dst_g = dst.rearrange("(q t p) d -> q p t d", t=TPG, p=P)
        ctx_g = ctxt.rearrange("(q t p) d -> q p t d", t=TPG, p=P)
        kv = 1 if cross else 0

        def dram(ap, idx):
            m, k = idx
            q = m * GPB + k
            return ap[q] if isinstance(q, int) else ap[bass.ds(q, 1)].rearrange("o p t d -> (o p) t d")

        turned_maxima = [] if ret else [(e_Qm, "tile", -1)]
        uses = {MA: {"inputs": [(e_xTs, "group", 0)], "V": [(e_V32, "group", 0), (e_gate, "group", 0)] if ret
                     else [(e_Vl, "group", 0)], "result": [(e_OTs, "group", -3)], "K0": [(e_Ks[0], "group", 0)],
                     "K1": [(e_Ks[1], "group", 0)], "maxima": turned_maxima},
                MB: {"QK": [(e_lo, "group", 0)], "maxima": [] if ret else [(e_Qm, "tile", -2)], "Q0": [(e_Qs[0], "group", 0)],
                     "Q1": [(e_Qs[1], "group", 0)], "out": [(e_r, "group", -3)]}}

        def bank_free(which, use, m, k, steps):
            names = [n_ for n_ in uses[which] if uses[which][n_]]
            i = names.index(use)
            for back in range(1, len(names) + 1):
                c = k // TPG - (1 if back > i else 0)
                found = False
                for ev, of, lag in uses[which][names[i - back]]:
                    j = c + lag if of == "group" else TPG * c + lag
                    per, total = (GPB, NQ) if of == "group" else (TPB, NT)
                    if steps is None or 0 <= m * per + j < total:
                        ev.wait(pe, (m, j))
                        found = True
                if found:
                    return

        def load(q):
            p = q[1] % 2
            y_before = (q[0], q[1] - 2)
            e_xb.wait(sp, (q[0], q[1] - 4))
            e_xT.wait(sp, (q[0], q[1] - 4))
            ld.mark(sp.dma_start(xg[q[1] % 4][:, :, :], dram(src_g, q)), q)
            if cross:
                e_xT.wait(sp, y_before)
                ldc.mark(sp.dma_start(cg[p][:, :, :], dram(ctx_g, q)), q)

        def turn_inputs(q, free):
            p = q[1] % 2
            free("inputs")
            ld.wait(pe, q)
            for t in range(TPG):
                i = pe.transpose(bankA[:, t * P:(t + 1) * P], xg[q[1] % 4][:, t, :], ident[:, :])
            if cross:
                ldc.wait(pe, q)
                for t in range(TPG):
                    i = pe.transpose(bankA[:, GT + t * P:GT + (t + 1) * P], cg[p][:, t, :], ident[:, :])
            e_xT.mark(i, q)
            e_V.wait(act, (q[0], q[1] - 2))
            e_xT.wait(act, q)
            n = 1 + kv
            e_xTs.mark(act.copy(srcT[p][:, 0:n, :].rearrange("p a t -> p (a t)"), bankA[:, 0:n * GT]), q)
            if causal:
                e_r.wait(act, (q[0], q[1] - 4))
                e_xb.mark(act.copy(xb[q[1] % 4][:, :, :].rearrange("p t d -> p (t d)"),
                                   xg[q[1] % 4][:, :, :].rearrange("p t d -> p (t d)")), q)
            else:
                e_r.wait(pool, (q[0], q[1] - 4))
                ld.wait(pool, q)
                e_xb.mark(pool.tensor_tensor(xb[q[1] % 4][:, :, :], xg[q[1] % 4][:, :, :],
                                               brow("a_bo" if ret else "x_bo"), ALU.add), q)

        def project_qk(q, free):
            p = q[1] % 2
            free("QK")
            e_xTs.wait(pe, q)
            pe.matmul(bankB[:, 0:GT], WQ, srcT[p][:, 0, :], start=True, stop=True)
            e_QK.mark(pe.matmul(bankB[:, GT:2 * GT], WK, srcT[p][:, kv, :], start=True, stop=True), q)
            e_sel[1].wait(act, (q[0], q[1] - 2))
            e_QK.wait(act, q)
            act.activation(hilo[p][:, 0, :], bankB[:, 0:GT], ACT.Identity, bias=column(bq))
            e_hi.mark(act.activation(hilo[p][:, 2, :], bankB[:, GT:2 * GT], ACT.Identity, bias=column(bk)), q)
            e_hi.wait(dve, q)
            dve.scalar_tensor_tensor(out=hilo[p][:, 1, :], in0=bankB[:, 0:GT], scalar=column(bq),
                                     in1=hilo[p][:, 0, :], op0=ALU.add, op1=ALU.subtract)
            e_lo.mark(dve.scalar_tensor_tensor(out=hilo[p][:, 3, :], in0=bankB[:, GT:2 * GT], scalar=column(bk),
                                                 in1=hilo[p][:, 2, :], op0=ALU.add, op1=ALU.subtract), q)

        def project_v(q, free):
            p = q[1] % 2
            free("V")
            for t in range(TPG):
                i = pe.matmul(bankA[:, t * P:(t + 1) * P], srcT[p][:, kv, t * P:(t + 1) * P], WV,
                              start=True, stop=True)
            if ret:
                i = pe.matmul(bankA[:, GT:2 * GT], W[:, w0 + 4, :], srcT[p][:, 0, :], start=True, stop=True)
            e_V.mark(i, q)

            def parts(v):
                return v.rearrange("p t (j e) -> p t j e", e=2 * DH)

            tiles_before = (q[0], TPG * (q[1] - 4) + TPG - 1)
            e_PV.wait(act, tiles_before)
            vh = Vh[q[1] % 4][:, :, :, 0:2 * DH]
            vp = bankA[:, 0:GT].rearrange("p (t j e) -> p t j e", t=TPG, e=2 * DH)
            if ret:
                e_V.wait(dve, q)
                e_V32.mark(dve.tensor_tensor(V32[p][:, :, :], bankA[:, 0:GT].rearrange("p (t d) -> p t d", t=TPG),
                                               brow("a_bv"), ALU.add), q)
                e_V32.wait(act, q)
                vp = V32[p][:, :, :].rearrange("p t (j e) -> p t j e", e=2 * DH)
                e_OTg.wait(act, (q[0], q[1] - 4))
                e_gate.mark(act.activation(GTs[q[1] % 4][:, :], bankA[:, GT:2 * GT], ACT.Sigmoid, bias=column("a_bg")), q)
            e_V.wait(act, q)
            for t in range(TPG):
                i = act.copy(vh[:, t], vp[:, t])
            e_Vh.mark(i, q)
            e_Vh.wait(dve, q)
            for t in range(TPG):
                i = dve.tensor_tensor(Vl[q[1] % 4][:, t], vp[:, t], vh[:, t], ALU.subtract)
            e_Vl.mark(i, q)

        def stack(q, j, free):
            p = q[1] % 2
            e_lo.wait(pe, q)
            free[f"Q{j}"](f"Q{j}")
            for g in (2 * j, 2 * j + 1):
                o = bankB[:, (g % 2) * GT:(g % 2 + 1) * GT]
                pe.matmul(o, sel[:, 0, g, :], hilo[p][:, 0, :], start=True, stop=False)
                pe.matmul(o, sel[:, 1, g, :], hilo[p][:, 1, :], start=False, stop=True)
            free[f"K{j}"](f"K{j}")
            for g in (2 * j, 2 * j + 1):
                o = bankA[:, (g % 2) * GT:(g % 2 + 1) * GT]
                pe.matmul(o, sel[:, 2, g, :], hilo[p][:, 2, :], start=True, stop=False)
                i = pe.matmul(o, sel[:, 3, g, :], hilo[p][:, 3, :], start=False, stop=True)
            e_sel[j].mark(i, q)
            tiles_before = (q[0], TPG * (q[1] - 2) + TPG - 1)
            for e in (act, dve):
                e_T.wait(e, tiles_before)
            e_sel[j].wait(act, q)
            e_Qs[j].mark(act.copy(Qst[p][:, 2 * j:2 * j + 2, :].rearrange("p g t -> p (g t)"), bankB[:, :]), q)
            e_sel[j].wait(dve, q)
            e_Ks[j].mark(dve.tensor_scalar(Kst[p][:, 2 * j:2 * j + 2, :].rearrange("p g t -> p (g t)"), bankA[:, :],
                                             column("ones_row"), None, ALU.add), q)

        def group_of(n):
            return (n[0], n[1] // TPG)

        def score_tile(n, strips, banks, left, left_at, right, right_at, mask):
            if mask is not None:
                for h in range(2):
                    pe.matmul(bank[:, banks + h, :].rearrange("p (k s) -> p k s", k=8), ident_b[:, :],
                              mask.unsqueeze(1).broadcast_to([P, 8, S]), start=True, stop=False, skip_group_check=True)
            for i in range(4):
                if i >= 2:
                    strips[i - 2].wait(pe, n)
                for g in range(NG):
                    slot = 2 * g + i // 2
                    for b in range(2):
                        inst = pe.matmul(bank[64 * b:64 * b + 64, banks + i % 2, slot * S:(slot + 1) * S],
                                         left[32 * i:32 * i + 32, g, left_at + b * S:left_at + (b + 1) * S],
                                         right[32 * i:32 * i + 32, g, right_at + b * S:right_at + (b + 1) * S],
                                         start=mask is None, stop=True, skip_group_check=mask is not None)
                if i < 2:
                    strips[i].mark(inst, n)
            return inst

        def scores_s(n):
            q, p, t = group_of(n), group_of(n)[1] % 2, n[1] % 2
            if t == 0:
                e_Qs[1].wait(pe, q)
                e_Ks[1].wait(pe, q)
            e_mx.wait(pe, (n[0], n[1] - 1))
            at = (n[1] % TPG) * P
            e_S.mark(score_tile(n, e_Si, S_BANK, Qst[p], at, Kst[p], at, masks_b[:, 1, :] if causal else None), n)

        def maxima(n):
            e_S.wait(dve, n)
            e_mT.wait(dve, (n[0], n[1] - 2))
            t = n[1] % 2
            full = mx[t][:, :, :].rearrange("p g (k h c) -> p h (g k) c", k=2, h=2, c=32)[:, :, :, MAX_ROW]
            e_mx.mark(dve.tensor_reduce(full, bank[:, S_BANK:S_BANK + 2, :].rearrange("p h (k s) -> p h k s", s=S),
                                          AX_X, ALU.max, negate=True), n)

        def turn_maxima(n, free):
            t = n[1] % 2
            in_bank = bankA if t else bankB
            free("maxima")
            e_mx.wait(pe, n)
            for g in range(NG):
                i = pe.matmul(in_bank[:, g * P:(g + 1) * P], mx[t][:, g, :], ident16[:, :], start=True, stop=True)
            e_mT.mark(i, n)
            q = group_of(n)
            at = (n[1] % TPG) * P
            e_T.wait(dve, (n[0], n[1] - 2))
            e_mT.wait(dve, n)
            e_Qm.mark(dve.tensor_tensor(Qm[t][:, :, :], in_bank[:, :].rearrange("p (g s) -> p g s", g=NG),
                                          Qst[q[1] % 2][:, :, at:at + P], ALU.add), n)

        def scores_t(n):
            q, p, t = group_of(n), group_of(n)[1] % 2, n[1] % 2
            at = (n[1] % TPG) * P
            tb = (S_BANK if t else T_BANK) if ret else T_BANK
            if ret:
                if t == 0:
                    e_Qs[1].wait(pe, q)
                    e_Ks[1].wait(pe, q)
                e_P.wait(pe, (n[0], n[1] - 2))
                right, right_at = Qst[p], at
            else:
                e_Qm.wait(pe, n)
                e_P.wait(pe, (n[0], n[1] - 1))
                right, right_at = Qm[t], 0
            e_T.mark(score_tile(n, e_Ti, tb, Kst[p], at, right, right_at, masks_b[:, 0, :] if causal else None), n)
            e = dve if ret else act
            e_T.wait(e, n)
            e_PV.wait(e, (n[0], n[1] - 2))
            e_Pl.wait(e, (n[0], n[1] - 2))
            sc = bank[:, tb:tb + 2, :].rearrange("p h (k s) -> p (h k) s", s=S)
            if ret:
                e_P.mark(dve.tensor_tensor(P32[t][:, :, :], sc, decay.unsqueeze(1).broadcast_to([P, H, S]),
                                             ALU.mult), n)
            else:
                e_P.mark(act.activation(P32[t][:, :, :], sc, ACT.Exp, scale=SCALE), n)

        def upper(t):
            return P32[t][:, :, :].rearrange("p k s -> p (k s)").bitcast(BF16)[:, 1::2]

        def weights_lo(n):
            t = n[1] % 2
            e_P.wait(pool, n)
            e_PV.wait(pool, (n[0], n[1] - 2))
            e_Pl.mark(pool.tensor_tensor(Plo[t][:, :, :].rearrange("p k s -> p (k s)"),
                                           P32[t][:, :, :].rearrange("p k s -> p (k s)"), upper(t), ALU.subtract), n)

        def weighted_sums(n):
            q, p, t, tt = group_of(n), group_of(n)[1] % 2, n[1] % 2, n[1] % TPG
            nv = 2 * DH if ret else 2 * DH + 1
            e_Vl.wait(pe, q)
            e_O.wait(pe, (n[0], n[1] - 1))
            e_P.wait(pe, n)
            e_Pl.wait(pe, n)
            up = upper(t)
            lo = Plo[t][:, :, :].rearrange("p k s -> p (k s)")
            for b in range(2):
                rows_b = slice(64 * b, 64 * b + 64)
                for j in range(PAIRS):
                    c = slice(j * P, (j + 1) * P)
                    o = bank[:, PV_BANK + b, j * 32:j * 32 + nv]
                    pe.matmul(o, up[rows_b, c], Vh[q[1] % 4][rows_b, tt, j, 0:nv], start=True, stop=False)
                    pe.matmul(o, lo[rows_b, c], Vh[q[1] % 4][rows_b, tt, j, 0:nv], start=False, stop=False)
                    i = pe.matmul(o[:, 0:2 * DH], up[rows_b, c], Vl[q[1] % 4][rows_b, tt, j, :], start=False, stop=True)
            e_PV.mark(i, n)
            pv = bank[:, PV_BANK:PV_BANK + 2, 0:PAIRS * 32].rearrange("p b (j c) -> p b j c", c=32)
            e_OT.wait(dve, (q[0], q[1] - 2)) if not ret else e_On.wait(dve, (q[0], q[1] - 2))
            e_PV.wait(dve, n)
            if not ret:
                e_rd.mark(dve.reciprocal(rden[t][:, :, :], pv[:, :, :, 2 * DH]), n)
                e_rd.wait(dve, n)
            ov = O[p][:, tt, :].rearrange("p (j i e) -> p j i e", i=2, e=DH)
            for b in range(2):
                for i2 in range(2):
                    rs_ = slice(64 * i2, 64 * i2 + 64)
                    o = ov[64 * b:64 * b + 64, :, i2, :]
                    a = pv[rs_, b, :, i2 * DH:(i2 + 1) * DH]
                    if ret:
                        i = dve.tensor_copy(o, a)
                    else:
                        i = dve.tensor_tensor(o, a, rden[t][rs_, b, :].unsqueeze(2).broadcast_to([64, PAIRS, DH]),
                                              ALU.mult)
            e_O.mark(i, n)

        def norm_scalars(q, j, v, evs, ready):
            p = q[1] % 2
            s1, s2, s3, s4 = evs
            ready(dve)
            for t in range(TPG):
                i = dve.bn_stats(st[j][p][:, t, :], v[:, t, :])
            s1.mark(i, q)
            s1.wait(dve, q)
            carrier()
            for t in range(TPG):
                i = dve.bn_aggr(mv[j][p][:, t, :], st[j][p][:, t, :])
            s2.mark(i, q)
            s2.wait(dve, q)
            s3.mark(dve.tensor_scalar(ve[j][p][:, :, 0], mv[j][p][:, :, 1], EPS, None, ALU.add), q)
            s3.wait(pool, q)
            s4.mark(pool.tensor_tensor(rstd[j][p][:, :, 0], ve[j][p][:, :, 0], minus_half[:, :], ALU.pow), q)

        def normalise(q, j, o, v, rs, ev):
            p = q[1] % 2
            rs.wait(dve, q)
            for t in range(TPG):
                i = dve.tensor_scalar(o[:, t, :], v[:, t, :], mv[j][p][:, t, 0:1], rstd[j][p][:, t, :],
                                      ALU.subtract, ALU.mult)
            ev.mark(i, q)

        def retained_scalars(q):
            last = (q[0], TPG * q[1] + TPG - 1)
            norm_scalars(q, 0, O[q[1] % 2], (e_st, e_mv, e_ve, e_rs), lambda e: e_O.wait(e, last))

        def norm_retained(q):
            e_OT.wait(dve, (q[0], q[1] - 2))
            normalise(q, 0, On[q[1] % 2], O[q[1] % 2], e_rs, e_On)

        def turn_result(q, free):
            p = q[1] % 2
            free("result")
            if ret:
                e_On.wait(pe, q)
                v = On[p]
            else:
                e_O.wait(pe, (q[0], TPG * q[1] + TPG - 1))
                v = O[p]
            for t in range(TPG):
                i = pe.transpose(bankA[:, t * P:(t + 1) * P], v[:, t, :], ident[:, :])
            e_OT.mark(i, q)
            before = (q[0], q[1] - 2)
            if ret:
                e_OTg.wait(dve, before)
                e_OT.wait(dve, q)
                e_OTs.mark(dve.tensor_scalar(OT[p][:, :], bankA[:, 0:GT], column("a_gamma"), column("a_beta"),
                                               ALU.mult, ALU.add), q)
                e_OTs.wait(dve, q)
                e_gate.wait(dve, q)
                e_out.wait(dve, before)
                e_OTg.mark(dve.tensor_tensor(OTg[p][:, :], OT[p][:, :], GTs[q[1] % 4][:, :], ALU.mult), q)
            else:
                e_out.wait(act, before)
                e_OT.wait(act, q)
                e_OTs.mark(act.activation(OT[p][:, :], bankA[:, 0:GT], ACT.Identity,
                                            bias=column("x_bv" if cross else "k_zero")), q)

        def project_out(q, free):
            p = q[1] % 2
            src_t = OTg[p] if ret else OT[p]
            free("out")
            (e_OTg if ret else e_OTs).wait(pe, q)
            for t in range(TPG):
                i = pe.matmul(bankB[:, t * P:(t + 1) * P], src_t[:, t * P:(t + 1) * P], WO, start=True, stop=True)
            e_out.mark(i, q)
            e_out.wait(dve, q)
            e_xb.wait(dve, q)
            e_y.wait(dve, (q[0], q[1] - 2))
            e_r.mark(dve.tensor_tensor(r[p][:, :, :], bankB[:, 0:GT].rearrange("p (t d) -> p t d", t=TPG),
                                         xb[q[1] % 4][:, :, :], ALU.add), q)
            norm_scalars(q, 1, r[p], (f_st, f_mv, f_ve, f_rs), lambda e: e_r.wait(e, q))

        def finish(q):
            p = q[1] % 2
            sto.wait(dve, (q[0], q[1] - 2))
            if not causal:
                normalise(q, 1, y[p], r[p], f_rs, e_y)
                return
            e_hn.wait(dve, (q[0], q[1] - 2))
            normalise(q, 1, hn[p], r[p], f_rs, e_hn)
            e_hn.wait(pool, q)
            e_hg.mark(pool.tensor_tensor(hg[p][:, :, :], hn[p][:, :, :], brow("g1"), ALU.mult), q)
            e_hg.wait(pool, q)
            sto.wait(pool, (q[0], q[1] - 2))
            e_y.mark(pool.tensor_tensor(y[p][:, :, :], hg[p][:, :, :], brow("b1"), ALU.add), q)

        def store(q):
            e_y.wait(act, q)
            sto.mark(act.dma_start(dram(dst_g, q), y[q[1] % 2][:, :, :]), q)

        def step(m, k, steps):

            def tile(lag):
                s = None if steps is None else steps - lag
                return (m, k - lag), s is None or 0 <= s < NT

            def group(lag):
                s = None if steps is None else (steps - lag) // TPG
                return (m, (k - lag) // TPG), s is None or 0 <= s < NQ

            def free_a(use):
                bank_free(MA, use, m, k, steps)

            def free_b(use):
                bank_free(MB, use, m, k, steps)

            q, on_q = group(k % 2)
            n_s, on_s = tile(2)
            n_t, on_t = tile(2 if ret else 3)
            n_w, on_w = tile(3 if ret else 4)
            q_o, on_o = group(6 + k % 2)
            if k % 2 == 0:
                q_f, on_f = group(8)
                if on_q:
                    load(q)
                    turn_inputs(q, free_a)
                if on_f:
                    finish(q_f)
                if not ret and on_s:
                    scores_s(n_s)
                    maxima(n_s)
                if ret and on_o:
                    norm_retained(q_o)
                if on_q:
                    project_qk(q, free_b)
                if ret and on_t:
                    scores_t(n_t)
                if on_w:
                    weighted_sums(n_w)
                if on_q:
                    project_v(q, free_a)
                if not ret and on_s:
                    turn_maxima(n_s, free_b)
                if not ret and on_t:
                    scores_t(n_t)
                if on_t:
                    weights_lo(n_t)
                if on_o:
                    turn_result(q_o, free_a)
            else:
                q_r, on_r = group(5)
                q_f, on_f = group(9)
                if on_f:
                    store(q_f)
                if on_q:
                    stack(q, 0, {"Q0": free_b, "K0": free_a})
                if not ret and on_s:
                    scores_s(n_s)
                    maxima(n_s)
                if ret and on_t:
                    scores_t(n_t)
                if ret and on_r:
                    retained_scalars(q_r)
                if on_q:
                    stack(q, 1, {"Q1": free_b, "K1": free_a})
                if on_w:
                    weighted_sums(n_w)
                if on_o:
                    project_out(q_o, free_b)
                if not ret and on_s:
                    turn_maxima(n_s, free_a)
                if not ret and on_t:
                    scores_t(n_t)
                if on_t:
                    weights_lo(n_t)

        for k in range(TPB):
            step(0, k, k)
        with nc.Fori(1, NB) as m:
            for k in range(TPB):
                step(m, k, None)
        for k in range(TPB):
            step(NB, k, NB * TPB + k)
        for k in (GPB - 2, GPB - 1):
            sto.wait(sp, (NB - 1, k))
        barrier()
        for e in events:
            if e not in unused:
                e.happened(NB)


    def moe_phase(h_src, x_src, dst):
        attention_ctx.close()
        free.extend(events)
        events.clear()
        ixd = U32
        h_t = [sb(f"h_t{p}", [P, MT, P]) for p in range(2)]
        x_t = [sb(f"x_t{p}", [P, MT, P]) for p in range(2)]
        ya_t = [sb(f"ya_t{p}", [P, MT, P]) for p in range(2)]
        yb_t = [sb(f"yb_t{p}", [P, MT, P]) for p in range(2)]
        hT = [sb(f"hT{p}", [P, MT * P]) for p in range(2)]
        lg = sb("lg", [P, NT, E_N])
        lg2 = sb("lg2", [P, NT, E_N])
        eq = sb("eq", [P, NT, E_N])
        pr = sb("pr", [P, NT, E_N])
        m12 = sb("m12", [P, 2, NT])
        r12 = sb("r12", [P, 2, NT])
        oh = sb("oh", [P, E_N, 2, NT])
        spread = sb("spread", [P, E_N, U])
        slot2 = sb("slot2", [P, E_N, U])
        tot = sb("tot", [P, E_N])
        cmp_ = sb("cmp_", [P, E_N, NT])
        cmpb = sb("cmpb", [P, NBLK, E_N - 1])
        nb = sb("nb", [P, E_N])
        pre = [sb(f"pre{j}", [P, 2 * E_N]) for j in range(4)]
        start = sb("start", [P, E_N])
        slotf = sb("slotf", [P, U])
        slots = sb("slots", [P, U], U32)
        ebf = sb("ebf", [P, NBLK])
        expert_of = sb("expert_of", [P, NBLK], mybir.dt.int32)
        d12 = sb("d12", [P, NT])
        e12 = sb("e12", [P, NT])
        s12 = sb("s12", [P, NT])
        wa = sb("wa", [P, NT])
        wb = sb("wb", [P, NT])
        hx = [sb(f"hx{p}", [P, 2, RW]) for p in range(4)]
        ix = [sb(f"ix{p}", [P, 2], ixd) for p in range(4)]
        xrow = [sb(f"xrow{p}", [P, RW]) for p in range(4)]
        ix2 = [sb(f"ix2_{p}", [P, 1], ixd) for p in range(4)]
        hTb = [sb(f"hTb{p}", [P, P]) for p in range(2)]
        we = [sb(f"we{p}", [P, WW]) for p in range(4)]
        G = [sb(f"G{p}", [P, FC, P]) for p in range(4)]
        yo = [sb(f"yo{p}", [P, P]) for p in range(2)]
        acc = [sb(f"acc{p}", [P, MT, P]) for p in range(2)]
        xb2 = [sb(f"xb2_{p}", [P, MT, P]) for p in range(2)]
        t1 = [sb(f"t1_{p}", [P, MT, P]) for p in range(2)]
        t2 = [sb(f"t2_{p}", [P, MT, P]) for p in range(2)]
        t3 = [sb(f"t3_{p}", [P, MT, P]) for p in range(2)]
        res = [sb(f"res{p}", [P, MT, P]) for p in range(2)]
        mst = [sb(f"mst{p}", [P, MT, 6]) for p in range(4)]
        mmv = [sb(f"mmv{p}", [P, MT, 2]) for p in range(4)]
        mve = [sb(f"mve{p}", [P, MT]) for p in range(4)]
        mrs = [sb(f"mrs{p}", [P, MT]) for p in range(4)]
        mh4 = sb("mh4", [P, MT])
        by_tile = h_src.rearrange("(t p) d -> t p d", p=P)
        by_block = buf.rearrange("(b p) w -> b p w", p=P)

        def item(ap, i):
            if isinstance(i, int):
                return ap[i]
            letters = " ".join("abcd"[:len(ap.shape) - 2])
            return ap[bass.ds(i, 1)].rearrange(f"o p {letters} -> (o p) {letters}")

        def at(idx, per):
            return idx[0] * per + idx[1]

        def columns(i, n):
            return slice(i, i + n) if isinstance(i, int) else bass.ds(i, n)

        def pool_carrier():
            carriers[1] += 1
            return pool.tensor_tensor(junk_p[:, carriers[1]:carriers[1] + 1], minus_half[:, 0:1], minus_half[:, 0:1], ALU.add)

        def pipeline(per, bodies, depth, step):
            for k in range(per):
                step(0, k, k)
            with nc.Fori(1, bodies) as m:
                for k in range(per):
                    step(m, k, None)
            for k in range(depth):
                step(bodies, k, bodies * per + k)

        def over(bodies):
            barrier()
            for e_ in events:
                e_.happened(bodies)
            free.extend(events)
            events.clear()

        def lagged(m, k, steps, lag, total):
            s = None if steps is None else steps - lag
            return (m, k - lag), s is None or 0 <= s < total

        r_ld = event("r_ld", 2, 16)
        r_hT, r_hTs, r_lg, r_lgs = (event(n, 2) for n in ("r_hT", "r_hTs", "r_lg", "r_lgs"))
        h_by_step = h_src.rearrange("(q t p) d -> q p t d", t=MT, p=P)
        x_by_step = x_src.rearrange("(q t p) d -> q p t d", t=MT, p=P)
        o_by_step = dst.rearrange("(q t p) d -> q p t d", t=MT, p=P)

        pool.memset(mh4[:, :], -0.5).then_inc(s_set, 1)
        pool.memset(ones[:, :], 1.0).then_inc(s_set, 1)
        pool.memset(pre[0][:, 0:E_N], 0.0).then_inc(s_set, 1)
        pool.memset(pre[1][:, 0:E_N], 0.0).then_inc(s_set, 1)
        pool.memset(pre[2][:, 0:E_N], 0.0).then_inc(s_set, 1)
        for e in (pe, dve, act, pool):
            e.wait_ge(s_w, moe_loads)
            e.wait_ge(s_set, 16)

        def router(m, k, steps):
            s0, on0 = lagged(m, k, steps, 0, NS)
            s1, on1 = lagged(m, k, steps, 1, NS)
            if on0:
                p = s0[1] % 2
                before = (s0[0], s0[1] - 2)
                r_hT.wait(sp, before)
                r_ld.mark(sp.dma_start(h_t[p][:, :, :], item(h_by_step, at(s0, 2))), s0)
                r_ld.wait(pe, s0)
                r_hTs.wait(pe, before)
                for t in range(MT):
                    i = pe.transpose(bank[:, p, t * P:(t + 1) * P], h_t[p][:, t, :], ident[:, :])
                r_hT.mark(i, s0)
                r_lg.wait(act, before)
                r_hT.wait(act, s0)
                r_hTs.mark(act.copy(hT[p][:, :], bank[:, p, :]), s0)
            if on1:
                p = s1[1] % 2
                r_hTs.wait(pe, s1)
                r_lgs.wait(pe, (s1[0], s1[1] - 2))
                for t in range(MT):
                    i = pe.matmul(bank[:, 2 + p, t * E_N:(t + 1) * E_N], hT[p][:, t * P:(t + 1) * P], wg_sb[:, :],
                                  start=True, stop=True)
                r_lg.mark(i, s1)
                r_lgs.wait(dve, (s1[0], s1[1] - 2))
                r_lg.wait(dve, s1)
                carrier()
                r_lgs.mark(dve.tensor_copy(lg[:, columns(at(s1, 2) * MT, MT), :],
                                           bank[:, 2 + p, 0:MT * E_N].rearrange("p (t e) -> p t e", e=E_N)), s1)

        pipeline(2, NS // 2, 1, router)
        for k in range(2):
            r_lgs.wait(dve, (NS // 2 - 1, k))
        over(NS // 2)

        s_dve = ctx.enter_context(nc.semaphore("s_dve"))
        s_pe = ctx.enter_context(nc.semaphore("s_pe"))
        s_act = ctx.enter_context(nc.semaphore("s_act"))
        n = [0]

        def chain(inst):
            n[0] += 1
            inst.then_inc(s_dve, 1)
            dve.wait_ge(s_dve, n[0])

        rev_b = rev[:, :].unsqueeze(1).broadcast_to([P, NT, E_N])
        for c, src_l in ((0, lg), (1, lg2)):
            ohv = oh[:, :, c, :].rearrange("p e t -> p t e")
            chain(dve.tensor_reduce(m12[:, c, :], src_l[:, :, :], AX_X, ALU.max))
            chain(dve.tensor_tensor(eq[:, :, :], src_l[:, :, :], m12[:, c, :].unsqueeze(2).broadcast_to([P, NT, E_N]),
                                    ALU.is_equal))
            chain(dve.tensor_tensor(pr[:, :, :], eq[:, :, :], rev_b, ALU.mult))
            chain(dve.tensor_reduce(r12[:, c, :], pr[:, :, :], AX_X, ALU.max))
            chain(dve.tensor_tensor(ohv, rev_b, r12[:, c, :].unsqueeze(2).broadcast_to([P, NT, E_N]), ALU.is_equal))
            if c == 0:
                chain(dve.scalar_tensor_tensor(out=lg2[:, :, :], in0=ohv, scalar=-1e30, in1=lg[:, :, :],
                                               op0=ALU.mult, op1=ALU.add))
        pe.wait_ge(s_dve, n[0])
        for e in range(E_N):
            i = pe.matmul(bank[0:U, 0, e:e + 1], oh[:, e, :, :].rearrange("p c t -> p (c t)"), ones[:, 0:1],
                          start=True, stop=True)
        i.then_inc(s_pe, 1)
        chain(dve.tensor_tensor(d12[:, :], m12[:, 1, :], m12[:, 0, :], ALU.subtract))
        act.wait_ge(s_dve, n[0])
        act.activation(e12[:, :], d12[:, :], ACT.Exp).then_inc(s_act, 1)
        dve.wait_ge(s_pe, 1)
        chain(dve.tensor_copy(tot[0:U, :], bank[0:U, 0, 0:E_N]))
        chain(dve.tensor_tensor(spread[0:U, :, :], tri[0:U, 0:U].unsqueeze(1).broadcast_to([U, E_N, U]),
                                tot[0:U, :].unsqueeze(2).broadcast_to([U, E_N, U]), ALU.mult))
        pe.wait_ge(s_dve, n[0])
        pe.matmul(bank[:, 1, 0:E_N], ones[0:U, :], tot[0:U, :], start=True, stop=True).then_inc(s_pe, 1)
        ohf = oh[:, :, :, :].rearrange("p e c t -> p (e c t)")
        spf = spread[:, :, :].rearrange("p e u -> p (e u)")
        half = E_N * U // 2
        for h in range(2):
            o = bank[:, 2 + h, 0:half]
            pe.matmul(o, tri[:, :], ohf[:, h * half:(h + 1) * half], start=True, stop=False)
            i = pe.matmul(o, ones[0:U, :], spf[0:U, h * half:(h + 1) * half], start=False, stop=True)
        i.then_inc(s_pe, 1)
        dve.wait_ge(s_pe, 2)
        chain(dve.tensor_tensor(cmp_[:, :, :], bank[:, 1, 0:E_N].unsqueeze(2).broadcast_to([P, E_N, NT]),
                                steps128[:, :].unsqueeze(1).broadcast_to([P, E_N, NT]), ALU.is_gt))
        chain(dve.tensor_reduce(pre[0][:, E_N:], cmp_[:, :, :], AX_X, ALU.add))
        for j in range(3):
            chain(dve.tensor_tensor(pre[j + 1][:, E_N:], pre[j][:, E_N:], pre[j][:, E_N - 2 ** j:2 * E_N - 2 ** j], ALU.add))
        last = pre[3][:, E_N:]
        chain(dve.tensor_tensor(nb[:, :], last, pre[0][:, E_N:], ALU.subtract))
        chain(dve.tensor_scalar(start[:, :], nb[:, :], float(P), None, ALU.mult))
        dve.wait_ge(s_pe, 3)
        for h in range(2):
            es = slice(h * E_N // 2, (h + 1) * E_N // 2)
            i = dve.tensor_tensor(slot2[:, es, :], bank[:, 2 + h, 0:half].rearrange("p (e u) -> p e u", u=U),
                                  start[:, es].unsqueeze(2).broadcast_to([P, E_N // 2, U]), ALU.add)
        chain(i)
        chain(dve.tensor_tensor(spread[:, :, :], slot2[:, :, :], oh[:, :, :, :].rearrange("p e c t -> p e (c t)"), ALU.mult))
        chain(dve.tensor_reduce(slotf[:, :], spread[:, :, :].rearrange("p e u -> p u e"), AX_X, ALU.add))
        chain(dve.tensor_copy(slots[:, :], slotf[:, :]))
        chain(dve.tensor_tensor(cmpb[:, :, :], last[:, 0:E_N - 1].unsqueeze(1).broadcast_to([P, NBLK, E_N - 1]),
                                blocks_row[:, :].unsqueeze(2).broadcast_to([P, NBLK, E_N - 1]), ALU.is_le))
        chain(dve.tensor_reduce(ebf[:, :], cmpb[:, :, :], AX_X, ALU.add))
        chain(dve.tensor_copy(expert_of[:, :], ebf[:, :]))
        dve.wait_ge(s_act, 1)
        chain(dve.tensor_scalar(s12[:, :], e12[:, :], 1.0, None, ALU.add))
        chain(dve.reciprocal(wa[:, :], s12[:, :]))
        chain(dve.tensor_tensor(wb[:, :], wa[:, :], e12[:, :], ALU.mult))

        d_ld = event("d_ld", BPB, 32, 4)
        d_ix = event("d_ix", BPB, 1, 4)
        d_sc = event("d_sc", BPB, 32, 4, fresh=True)
        pool.wait_ge(s_fill, 16)

        d_go = event("d_go", BPB, 1, 4)

        def dispatch(m, k, steps):
            t, on = lagged(m, k, steps, 0, NT)
            b = k % 4
            before = (t[0], t[1] - 4)
            d_sc.wait(sp, before)
            for c in range(2):
                sp.dma_start(hx[b][:, c, 0:P], item(by_tile, at(t, BPB))).then_inc(d_ld.at(t)[0], 16)
            d_sc.wait(dve, before)
            carrier()
            dve.tensor_copy(hx[b][:, :, P], ids[:, :, columns(at(t, BPB), 1)].rearrange("p c t -> p (c t)"))
            sl = slots[:, :].rearrange("p (c t) -> p c t", c=2)
            d_ix.mark(dve.tensor_copy(ix[b][:, :], sl[:, :, columns(at(t, BPB), 1)].rearrange("p c t -> p (c t)")), t)
            d_go.wait(pool, before)
            d_ld.wait(pool, t)
            pool_carrier()
            d_ix.wait(pool, t)
            d_go.mark(pool_carrier(), t)
            for c in range(2):
                pool.indirect_dma_start(buf[:, :], bass.IndirectOffsetOnAxis(ix[b][:, c:c + 1], 0), hx[b][:, c, :],
                                        None).then_inc(d_sc.at(t)[0], 16)

        pipeline(BPB, NT // BPB, 0, dispatch)
        for k in range(4):
            d_sc.wait(sp, (NT // BPB - 1, k))
        over(NT // BPB)

        b_ld = event("b_ld", EPB, 16, 4)
        b_xT, b_xTs, b_we, b_z, b_g, b_y, b_ix, b_yo = (event(n_, EPB) for n_ in
                                                  ("b_xT", "b_xTs", "b_we", "b_z", "b_g", "b_y", "b_ix", "b_yo"))
        b_sc = event("b_sc", EPB, 16, fresh=True)
        b_go = event("b_go", EPB)

        def expert(m, k, steps):
            s0, on0 = lagged(m, k, steps, 0, NBLK)
            s1, on1 = lagged(m, k, steps, 1, NBLK)
            s3, on3 = lagged(m, k, steps, 3, NBLK)
            if on3:
                p, b = s3[1] % 2, s3[1] % 4
                before = (s3[0], s3[1] - 2)
                b_g.wait(pe, s3)
                b_yo.wait(pe, before)
                for c in range(FC):
                    i = pe.matmul(bank[:, 4 + p, 0:P], G[b][:, c, :], we[b][:, W2 + c * P:W2 + (c + 1) * P],
                                  start=c == 0, stop=c == FC - 1)
                b_y.mark(i, s3)
                b_sc.wait(dve, before)
                b_y.wait(dve, s3)
                b_yo.mark(dve.tensor_tensor(yo[p][:, :], bank[:, 4 + p, 0:P], we[b][:, B2:B2 + P], ALU.add), s3)
                b_go.wait(pool, before)
                b_ix.wait(pool, s3)
                pool_carrier()
                b_yo.wait(pool, s3)
                b_go.mark(pool_carrier(), s3)
                b_sc.mark(pool.indirect_dma_start(ydst[:, :], bass.IndirectOffsetOnAxis(ix2[b][:, :], 0), yo[p][:, :],
                                                  None), s3)
            if on0:
                p, b = s0[1] % 2, s0[1] % 4
                before = (s0[0], s0[1] - 4)
                b_xT.wait(sp, before)
                b_ix.wait(sp, before)
                b_ld.mark(sp.dma_start(xrow[b][:, :], item(by_block, at(s0, EPB))), s0)
                b_ld.wait(pe, s0)
                b_xTs.wait(pe, (s0[0], s0[1] - 2))
                b_xT.mark(pe.transpose(bank[:, p, 0:P], xrow[b][:, 0:P], ident[:, :]), s0)
                b_z.wait(act, (s0[0], s0[1] - 2))
                b_xT.wait(act, s0)
                b_xTs.mark(act.copy(hTb[p][:, :], bank[:, p, 0:P]), s0)
                e = dve.value_load(expert_of[0:1, columns(at(s0, EPB), 1)], min_val=0, max_val=E_N - 1)
                b_y.wait(dve, before)
                b_g.wait(dve, before)
                b_yo.wait(dve, before)
                carrier()
                b_we.mark(dve.tensor_copy(we[b][:, :], wx[:, bass.ds(e, 1), :].rearrange("p o w -> p (o w)")), s0)
                b_ld.wait(dve, s0)
                b_sc.wait(dve, before)
                b_ix.mark(dve.tensor_scalar(ix2[b][:, :], xrow[b][:, P:P + 1], trash[:, p:p + 1], None, ALU.max), s0)
            if on1:
                p, b = s1[1] % 2, s1[1] % 4
                before = (s1[0], s1[1] - 2)
                b_xTs.wait(pe, s1)
                b_we.wait(pe, s1)
                b_g.wait(pe, before)
                for c in range(FC):
                    i = pe.matmul(bank[:, 2 + p, c * P:(c + 1) * P], we[b][:, W1 + c * P:W1 + (c + 1) * P],
                                  hTb[p][:, :], start=True, stop=True)
                b_z.mark(i, s1)
                b_y.wait(act, (s1[0], s1[1] - 4))
                b_we.wait(act, s1)
                b_z.wait(act, s1)
                for c in range(FC):
                    i = act.activation(G[b][:, c, :], bank[:, 2 + p, c * P:(c + 1) * P], ACT.Gelu_apprx_tanh,
                                       bias=we[b][:, B1 + c:B1 + c + 1])
                b_g.mark(i, s1)

        pipeline(EPB, NBLK // EPB, 3, expert)
        for k in range(2):
            b_sc.wait(sp, (NBLK // EPB - 1, EPB - 2 + k))
        over(NBLK // EPB)

        f_ld = event("f_ld", 2, 64)
        f_acc, f_t1, f_t2, f_t3, f_xb, f_res = (event(n_, 2) for n_ in ("g_acc", "g_t1", "g_t2", "g_t3", "g_xb", "g_res"))
        norms = [[event(f"g_{w_}{j}", 2) for w_ in ("st", "mv", "ve", "rs")] for j in range(2)]
        f_st_ = event("g_sto", 2, 16)
        y_by_step = [ydst[TRASH + c * T_N:TRASH + (c + 1) * T_N, :].rearrange("(q t p) d -> q p t d", t=MT, p=P)
                     for c in range(2)]

        def scalars(j, s, v, ready):
            p = s[1] % 2
            w = 2 * j + p
            st_, mv_, ve_, rs_ = norms[j]
            ready(dve)
            carrier()
            for t in range(MT):
                i = dve.bn_stats(mst[w][:, t, :], v[:, t, :])
            st_.mark(i, s)
            st_.wait(dve, s)
            carrier()
            for t in range(MT):
                i = dve.bn_aggr(mmv[w][:, t, :], mst[w][:, t, :])
            mv_.mark(i, s)
            mv_.wait(dve, s)
            ve_.mark(dve.tensor_scalar(mve[w][:, :], mmv[w][:, :, 1], EPS, None, ALU.add), s)
            ve_.wait(pool, s)
            rs_.mark(pool.tensor_tensor(mrs[w][:, :], mve[w][:, :], mh4[:, :], ALU.pow), s)

        def normed(j, s, o, v):
            p = s[1] % 2
            w = 2 * j + p
            norms[j][3].wait(dve, s)
            for t in range(MT):
                i = dve.tensor_scalar(o[:, t, :], v[:, t, :], mmv[w][:, t, 0:1], mrs[w][:, t:t + 1],
                                      ALU.subtract, ALU.mult)
            return i

        def br(name):
            return row[:, ROWS.index(name), :].unsqueeze(1).broadcast_to([P, MT, P])

        def combine(m, k, steps):
            s0, on0 = lagged(m, k, steps, 0, NS)
            s1, on1 = lagged(m, k, steps, 1, NS)
            s2, on2 = lagged(m, k, steps, 2, NS)
            if on0:
                p = s0[1] % 2
                before = (s0[0], s0[1] - 2)
                f_xb.wait(sp, before)
                at0 = at(s0, 2)
                for d_, s_ in ((h_t, h_by_step), (x_t, x_by_step), (ya_t, y_by_step[0]), (yb_t, y_by_step[1])):
                    sp.dma_start(d_[p][:, :, :], item(s_, at0)).then_inc(f_ld.at(s0)[0], 16)
            if on2:
                p = s2[1] % 2
                f_st_.wait(dve, (s2[0], s2[1] - 2))
                f_res.mark(normed(1, s2, res[p], t3[p]), s2)
                f_res.wait(act, s2)
                f_st_.mark(act.dma_start(item(o_by_step, at(s2, 2)), res[p][:, :, :]), s2)
            if on1:
                p = s1[1] % 2
                before = (s1[0], s1[1] - 2)
                f_t2.wait(dve, before)
                f_t1.mark(normed(0, s1, t1[p], acc[p]), s1)
                f_t3.wait(pool, before)
                f_t1.wait(pool, s1)
                f_t2.mark(pool.tensor_tensor(t2[p][:, :, :], t1[p][:, :, :], br("g2"), ALU.mult), s1)
            if on0:
                p = s0[1] % 2
                before = (s0[0], s0[1] - 2)
                f_t1.wait(dve, before)
                f_ld.wait(dve, s0)
                carrier()
                at0 = at(s0, 2) * MT
                for t in range(MT):
                    i = dve.scalar_tensor_tensor(out=acc[p][:, t, :], in0=ya_t[p][:, t, :], scalar=wa[:, columns(at0 + t, 1)],
                                                 in1=h_t[p][:, t, :], op0=ALU.mult, op1=ALU.add)
                f_half.mark(i, s0)
                f_half.wait(dve, s0)
                for t in range(MT):
                    i = dve.scalar_tensor_tensor(out=acc[p][:, t, :], in0=yb_t[p][:, t, :], scalar=wb[:, columns(at0 + t, 1)],
                                                 in1=acc[p][:, t, :], op0=ALU.mult, op1=ALU.add)
                f_acc.mark(i, s0)
                f_acc.wait(pool, s0)
                f_t3.wait(pool, before)
                f_xb.mark(pool.tensor_tensor(xb2[p][:, :, :], x_t[p][:, :, :], br("b2"), ALU.add), s0)
                scalars(0, s0, acc[p], lambda e: f_acc.wait(e, s0))
            if on1:
                p = s1[1] % 2
                f_xb.wait(dve, s1)
                f_t2.wait(dve, s1)
                f_res.wait(dve, (s1[0], s1[1] - 2))
                f_t3.mark(dve.tensor_tensor(t3[p][:, :, :], t2[p][:, :, :], xb2[p][:, :, :], ALU.add), s1)
                scalars(1, s1, t3[p], lambda e: f_t3.wait(e, s1))

        f_half = event("g_half", 2)
        pipeline(2, NS // 2, 2, combine)
        for k in range(2):
            f_st_.wait(sp, (NS // 2 - 1, k))

    xf = x.rearrange("b s d -> (b s) d")
    ctxt = ctxt.rearrange("b s d -> (b s) d")
    outf = out.rearrange("b s d -> (b s) d")
    targets = [x1, x2, hd]
    softmax_only = [e_S, *e_Si, e_mx, e_mT, e_Qm, e_rd]
    self_only = [e_hn, e_hg]
    retention_only = [e_V32, e_gate, e_OTg, e_st, e_mv, e_ve, e_rs, e_On]
    attention_phase("ret", xf, outf if upto == 1 else x1, [ldc, *softmax_only, *self_only])
    if upto >= 2:
        attention_phase("cross", x1, outf if upto == 2 else x2, [*retention_only, *self_only])
    if upto >= 3:
        attention_phase("self", x2, outf if upto == 3 else hd, [ldc, *retention_only])
    if upto >= 4:
        moe_phase(hd, x2, outf)
    return ctx, events


def lay_out(inputs):
    a = {k: np.asarray(v) for k, v in inputs.items()}
    A, X, N = (lambda n: a["L0_attn_" + n]), (lambda n: a["L0_xattn_" + n]), (lambda n: a["L0_ffn_" + n])
    ident, sel, masks, ones_row = shape_constants()
    qkv = N("w_qkv")
    wmats = np.stack([A("Wq"), A("Wk"), A("Wv"), A("Wo"), A("Wg"),
                      X("wq_w").T, X("wk_w").T, X("wv_w").T, X("wo_w").T,
                      qkv[:, 0:P], qkv[:, P:2 * P], qkv[:, 2 * P:], N("w_o")])
    cols = np.stack([A("bq"), A("bk"), A("bg"), A("gamma"), A("beta"), X("wq_b"), X("wk_b"), X("wv_b"),
                     ones_row, np.zeros(P, np.float32)], 1)
    rows = np.stack([A("bv"), A("bo"), X("wo_b"), N("g1"), N("b1"), N("g2"), N("b2")])
    c = np.ascontiguousarray
    return {"x": a["x"], "ctxt": a["ctx_1024"], "wmats": c(wmats), "cols": c(cols), "rows": c(rows),
            "const_ident": ident, "const_sel": sel, "const_masks": masks, **routing_constants(a["x"].shape[0] * S // P), "wg": N("wg"),
            "w1": N("w1"), "bb1t": c(N("bb1").reshape(E_N * FC, P).T), "w2": N("w2"), "bb2": N("bb2")}


def kernel(**inputs):
    import concourse.bacc as _bacc
    from concourse.bass_utils import run_bass_kernel_spmd as _run

    nc = _bacc.Bacc("TRN2", target_bir_lowering=False, num_devices=1)
    arrays = lay_out(inputs)
    args = {n: nc.dram_tensor(n, a.shape, mybir.dt.from_np(a.dtype), kind="ExternalInput").ap()
            for n, a in arrays.items()}
    out = nc.dram_tensor("out", arrays["x"].shape, F32, kind="ExternalOutput").ap()
    build(nc, **args, out=out)
    r = _run(nc, [arrays], core_ids=[0])
    return r.results[0]["out"]
```

```python
from contextlib import ExitStack

import numpy as np
import concourse.bass as bass
from concourse import mybir

F32 = mybir.dt.float32
F16 = mybir.dt.float16
BF16 = mybir.dt.bfloat16
U32 = mybir.dt.uint32
ALU = mybir.AluOpType
ACT = mybir.ActivationFunctionType
AX_X = mybir.AxisListType.X

P = 128
S = 64
H = 16
DH = 8
NG = 4
PAIRS = H // 2
TPG = 2
GT = TPG * P
TPB = 8
GPB = TPB // TPG
EPS = 1e-5
SCALE = DH ** -0.5
MAX_ROW = 24
E_N = 8
F_N = 512
FC = F_N // P

COLS = ["a_bq", "a_bk", "a_bg", "a_gamma", "a_beta", "x_bq", "x_bk", "x_bv", "ones_row", "k_zero"]
ROWS = ["a_bv", "a_bo", "x_bo", "g1", "b1", "g2", "b2"]


def head_of(g, i):
    return (i % 2) * 8 + 2 * g + i // 2


def shape_constants():
    ident = np.eye(P, dtype=np.float32)
    sel = np.zeros((P, 4, NG, P), np.float32)
    for g in range(NG):
        for i in range(4):
            for d in range(DH):
                src, row = head_of(g, i) * DH + d, 32 * i + d
                sel[src, 0, g, row] = sel[src, 0, g, row + 8] = sel[src, 1, g, row + 16] = 1
                sel[src, 2, g, row] = sel[src, 2, g, row + 16] = sel[src, 3, g, row + 8] = 1
    s = np.arange(P) % S
    diff = np.arange(S)[None, :] - s[:, None]
    decay = np.where(diff >= 0, np.power(np.float32(0.99), diff.astype(np.float32)), 0).astype(np.float32)
    decay = (decay * np.float32(SCALE)).astype(np.float32)
    mask_t = np.where(diff >= 0, 0, -1e30).astype(np.float32)
    mask_s = np.where(diff <= 0, 0, -1e30).astype(np.float32)
    ones_row = np.zeros(P, np.float32)
    ones_row[MAX_ROW::32] = 1
    return ident, sel.reshape(P, -1), np.concatenate([decay, mask_t, mask_s], 1), ones_row


def routing_constants(tiles):
    f, n = np.float32, tiles * P
    p = np.arange(P)[:, None]
    ids = 2 * P + np.arange(2)[None, :, None] * n + np.arange(tiles)[None, None] * P + p[:, :, None]
    return {"const_ids": ids.reshape(P, -1).astype(f), "const_tri": np.triu(np.ones((P, P), f), 1),
            "const_rev": (E_N - np.arange(E_N, dtype=f))[None], "const_steps": np.arange(tiles, dtype=f)[None] * P,
            "const_blocks": np.arange(2 * tiles + E_N, dtype=f)[None],
            "const_trash": (p + P * np.arange(2)[None]).astype(f)}


class Event:

    def __init__(self, sems, per_body, inc, origin=0):
        self.sems, self.turns, self.inc, self.origin = sems, len(sems), inc, origin
        self.rounds = per_body // self.turns

    def at(self, idx):
        m, k = idx
        return self.sems[k % self.turns], m * self.rounds + k // self.turns

    def mark(self, instruction, idx):
        instruction.then_inc(self.at(idx)[0], self.inc)
        return instruction

    def wait(self, engine, idx):
        sem, m = self.at(idx)
        k = idx[1]
        if isinstance(m, int) and m < 0:
            return
        assert isinstance(m, int) or self.rounds + k // self.turns + self.origin // self.inc + 1 > 0, (self.sems[0].name, idx)
        engine.wait_ge(sem, m * self.inc + (self.inc + self.origin))

    def happened(self, bodies):
        self.origin += bodies * self.rounds * self.inc


def build(nc, x, ctxt, wmats, cols, rows, const_ident, const_sel, const_masks, const_ids, const_tri, const_rev, const_steps, const_blocks, const_trash, wg, w1, bb1t, w2, bb2, out, upto=4):
    T_N = x.shape[0] * x.shape[1]
    NT = T_N // P
    NQ = NT // TPG
    NB = NT // TPB
    pe, dve, act, pool, sp = nc.tensor, nc.vector, nc.scalar, nc.gpsimd, nc.sync
    ctx = ExitStack()
    in_ctx = [ctx]

    def sb(name, shape, dt=F32):
        return in_ctx[-1].enter_context(nc.sbuf_tensor(name, shape, dt))

    def event(name, per_body, inc=1, turns=2, fresh=False):
        for old in free:
            if not fresh and (old.inc > 1) == (inc > 1) and old.turns == turns:
                free.remove(old)
                e = Event(old.sems, per_body, inc, old.origin)
                break
        else:
            e = Event([ctx.enter_context(nc.semaphore(f"{name}{r}")) for r in range(turns)], per_body, inc)
        e.fresh = fresh
        events.append(e)
        return e

    free = []
    events = []
    ident = sb("ident", [P, P])
    ident16 = sb("ident16", [P, P], F16)
    sel_f = sb("sel_f", [P, 4 * NG * P])
    sel = sb("sel", [P, 4, NG, P], F16)
    masks_f = sb("masks_f", [P, 3 * S])
    decay = masks_f[:, 0:S]
    W = sb("W", [P, wmats.shape[0], P])
    col = sb("col", [P, len(COLS)])
    row = sb("row", [P, len(ROWS), P])
    wg_sb = sb("wg_sb", [P, E_N])

    MT = 4
    NS = NT // MT
    U = 2 * NT
    NBLK = U + E_N
    BPB = 4
    EPB = 8
    RW = P + 1
    WW = 2 * F_N + FC + P
    W1, W2, B1, B2 = 0, F_N, 2 * F_N, 2 * F_N + FC
    TRASH = 2 * P
    buf = nc.dram_tensor("block_rows", (NBLK * P, RW), F32).ap()
    ydst = nc.dram_tensor("expert_rows", (TRASH + 2 * T_N, P), F32).ap()

    wx = sb("wx", [P, E_N, WW])
    zeros = sb("zeros", [P, RW])
    s_w = ctx.enter_context(nc.semaphore("s_w"))
    s_fill = ctx.enter_context(nc.semaphore("s_fill"))
    s_zero = ctx.enter_context(nc.semaphore("s_zero"))
    ids = sb("ids", [P, 2, NT])
    tri = sb("tri", [P, P])
    rev = sb("rev", [P, E_N])
    steps128 = sb("steps128", [P, NT])
    blocks_row = sb("blocks_row", [P, NBLK])
    trash = sb("trash", [P, 2])
    ones = sb("ones", [P, P])

    junk = sb("junk", [P, 256])
    junk_p = sb("junk_p", [P, 128])
    minus_half = sb("minus_half", [P, TPG])

    attention_ctx = ExitStack()
    in_ctx[0] = attention_ctx
    xg = [sb(f"xg{p}", [P, TPG, P]) for p in range(4)]
    cg = [sb(f"cg{p}", [P, TPG, P]) for p in range(2)]
    xb = [sb(f"xb{p}", [P, TPG, P]) for p in range(4)]
    srcT = [sb(f"srcT{p}", [P, 2, GT]) for p in range(2)]
    hilo = [sb(f"hilo{p}", [P, 4, GT], F16) for p in range(2)]
    Qst = [sb(f"Qst{p}", [P, NG, GT], F16) for p in range(2)]
    Kst = [sb(f"Kst{p}", [P, NG, GT], F16) for p in range(2)]
    V32 = [sb(f"V32_{p}", [P, TPG, P]) for p in range(2)]
    Vh = [sb(f"Vh{p}", [P, TPG, PAIRS, 2 * DH + 1], F16) for p in range(4)]
    Vl = [sb(f"Vl{p}", [P, TPG, PAIRS, 2 * DH], F16) for p in range(4)]
    GTs = [sb(f"GTs{p}", [P, GT]) for p in range(4)]
    mx = [sb(f"mx{t}", [P, NG, P], F16) for t in range(2)]
    Qm = [sb(f"Qm{t}", [P, NG, P], F16) for t in range(2)]
    Sm = sb("Sm", [P, H, S])
    Tm = [sb(f"Tm{t}", [P, H, S]) for t in range(2)]
    P32 = [sb(f"P32_{t}", [P, H, S]) for t in range(2)]
    Plo = [sb(f"Plo{t}", [P, H, S], F16) for t in range(2)]
    rden = [sb(f"rden{t}", [P, 2, PAIRS]) for t in range(2)]
    O = [sb(f"O{p}", [P, TPG, P]) for p in range(2)]
    On = [sb(f"On{p}", [P, TPG, P]) for p in range(2)]
    OT = [sb(f"OT{p}", [P, GT]) for p in range(2)]
    OTg = [sb(f"OTg{p}", [P, GT]) for p in range(2)]
    r = [sb(f"r{p}", [P, TPG, P]) for p in range(2)]
    y = [sb(f"y{p}", [P, TPG, P]) for p in range(2)]
    st, mv, ve, rstd = ([[sb(f"{n_}{j}{p}", [P, TPG, w_]) for p in range(2)] for j in range(2)]
                        for n_, w_ in (("st", 6), ("mv", 2), ("ve", 1), ("rstd", 1)))
    hn = [sb(f"hn{p}", [P, TPG, P]) for p in range(2)]
    hg = [sb(f"hg{p}", [P, TPG, P]) for p in range(2)]

    in_ctx[0] = ctx

    bank = ctx.enter_context(nc.psum_tensor("bank", [P, 8, 512], F32))
    S_BANK, T_BANK, PV_BANK, MA, MB = 0, 2, 4, 6, 7
    bankA, bankB = bank[:, MA, :], bank[:, MB, :]

    x1 = nc.dram_tensor("x1_scratch", (T_N, P), F32).ap()
    x2 = nc.dram_tensor("x2_scratch", (T_N, P), F32).ap()
    hd = nc.dram_tensor("h_scratch", (T_N, P), F32).ap()

    ld = event("ld", GPB, 16, 4)
    ldc = event("ldc", GPB, 16)
    sto = event("sto", GPB, 16)
    e_xT = event("xT", GPB)
    e_xTs = event("xTs", GPB)
    e_QK = event("QK", GPB)
    e_hi = event("hi", GPB)
    e_lo = event("lo", GPB)
    e_V = event("V", GPB)
    e_V32 = event("V32", GPB)
    e_Vh = event("Vh", GPB)
    e_Vl = event("Vl", GPB)
    e_gate = event("gate", GPB)
    e_sel = [event(f"sel{j}", GPB) for j in range(2)]
    e_Qs = [event(f"Qs{j}", GPB) for j in range(2)]
    e_Ks = [event(f"Ks{j}", GPB) for j in range(2)]
    e_S = event("S", TPB)
    e_Si = [event(f"Si{i}", TPB) for i in range(2)]
    e_Ti = [event(f"Ti{i}", TPB) for i in range(2)]
    e_Sm = event("Sm", TPB)
    e_Tm = event("Tm", TPB)
    e_mx = event("mx", TPB)
    e_mT = event("mT", TPB)
    e_Qm = event("Qm", TPB)
    e_T = event("T", TPB)
    e_P = event("P", TPB)
    e_Pl = event("Pl", TPB)
    e_PV = event("PV", TPB)
    e_rd = event("rd", TPB)
    e_O = event("O", TPB)
    e_xb = event("xb", GPB)
    e_st = event("st", GPB)
    e_mv = event("mv", GPB)
    e_ve = event("ve", GPB)
    e_rs = event("rs", GPB)
    e_On = event("On", GPB)
    f_st, f_mv, f_ve, f_rs = (event(n, GPB) for n in ("fst", "fmv", "fve", "frs"))
    e_OT = event("OT", GPB)
    e_OTs = event("OTs", GPB)
    e_OTg = event("OTg", GPB)
    e_out = event("out", GPB)
    e_r = event("r", GPB)
    e_y = event("y", GPB)
    e_hn = event("hn", GPB)
    e_hg = event("hg", GPB)
    s_ld = ctx.enter_context(nc.semaphore("s_ld"))
    s_set = ctx.enter_context(nc.semaphore("s_set"))
    s_bar = ctx.enter_context(nc.semaphore("s_bar"))
    barriers = [0]

    carriers = [0, 0]

    def carrier():
        carriers[0] += 1
        dve.memset(junk[:, carriers[0]:carriers[0] + 1], 0.0)

    def barrier():
        barriers[0] += 1
        for e in (pe, dve, act, pool, sp):
            e.drain().then_inc(s_bar, 1)
        for e in (pe, dve, act, pool, sp):
            e.wait_ge(s_bar, 5 * barriers[0])

    loads = 0
    for dst, src in ((ident[:, :], const_ident), (sel_f[:, :], const_sel), (masks_f[:, :], const_masks),
                     (W[:, :, :], wmats.rearrange("w p n -> p w n")), (col[:, :], cols),
                     (wg_sb[:, :], wg)):
        sp.dma_start(dst, src).then_inc(s_ld, 16)
        loads += 16
    for n in range(len(ROWS)):
        sp.dma_start(row[:, n, :], rows[n:n + 1, :].broadcast_to([P, P])).then_inc(s_ld, 16)
        loads += 16
    pool.memset(zeros[:, :], 0.0).then_inc(s_zero, 1)
    sp.wait_ge(s_zero, 1)
    for t in range(2):
        pool.memset(mx[t][:, :, :], 0.0).then_inc(s_set, 1)
    for t in range(4):
        pool.memset(Vh[t][:, :, :, :], 1.0).then_inc(s_set, 1)
    for e in (sto, e_OT, e_OTg, e_out, e_y, e_hn):
        for sem in e.sems:
            pool.sem_inc(sem, e.inc)
        e.origin = e.inc
    pool.memset(minus_half[:, :], -0.5).then_inc(s_set, 1)
    dve.wait_ge(s_ld, loads)
    dve.tensor_copy(ident16[:, :], ident[:, :]).then_inc(s_set, 1)
    dve.tensor_copy(sel[:, :, :, :].rearrange("p a g n -> p (a g n)"), sel_f[:, :]).then_inc(s_set, 1)
    for e in (pe, act, pool, dve):
        e.wait_ge(s_ld, loads)
        e.wait_ge(s_set, 9)

    moe_loads = 16 * (9 + E_N)

    def load_mixture():
        for dst_, src_ in ((wx[:, :, W1:W1 + F_N], w1.rearrange("e d f -> d e f")),
                           (wx[:, :, B1:B1 + FC], bb1t.rearrange("p (e c) -> p e c", c=FC)),
                           (wx[:, :, B2:B2 + P], bb2.rearrange("e d -> (e d)").unsqueeze(0).broadcast_to([P, E_N * P])
                            .rearrange("p (e d) -> p e d", d=P)),
                           (ids[:, :, :].rearrange("p c t -> p (c t)"), const_ids), (tri[:, :], const_tri),
                           (rev[:, :], const_rev.broadcast_to([P, E_N])),
                           (steps128[:, :], const_steps.broadcast_to([P, NT])),
                           (blocks_row[:, :], const_blocks.broadcast_to([P, NBLK])), (trash[:, :], const_trash)):
            sp.dma_start(dst_, src_).then_inc(s_w, 16)
        for e_ in range(E_N):
            sp.dma_start(wx[:, e_, W2:W2 + F_N].rearrange("f (c d) -> f c d", d=P),
                         w2[e_].rearrange("(c f) d -> f c d", f=P)).then_inc(s_w, 16)

    ZPB = NBLK // NB

    def clear_blocks(m):
        d = buf.rearrange("(m p j) w -> m p j w", p=P, j=ZPB)
        sp.dma_start(d[m] if isinstance(m, int) else d[bass.ds(m, 1)].rearrange("o p j w -> (o p) j w"),
                     zeros[:, :].unsqueeze(1).broadcast_to([P, ZPB, RW])).then_inc(s_fill, 16)

    def column(name):
        k = COLS.index(name)
        return col[:, k:k + 1]

    def brow(name):
        return row[:, ROWS.index(name), :].unsqueeze(1).broadcast_to([P, TPG, P])

    def attention_phase(kind, src, dst, unused):
        ret, cross, causal = kind == "ret", kind == "cross", kind == "self"
        w0 = {"ret": 0, "cross": 5, "self": 9}[kind]
        WQ, WK, WV, WO = (W[:, w0 + j, :] for j in range(4))
        bq = {"ret": "a_bq", "cross": "x_bq", "self": "k_zero"}[kind]
        bk = {"ret": "a_bk", "cross": "x_bk", "self": "k_zero"}[kind]
        src_g = src.rearrange("(q t p) d -> q p t d", t=TPG, p=P)
        dst_g = dst.rearrange("(q t p) d -> q p t d", t=TPG, p=P)
        ctx_g = ctxt.rearrange("(q t p) d -> q p t d", t=TPG, p=P)
        kv = 1 if cross else 0

        def dram(ap, idx):
            m, k = idx
            q = m * GPB + k
            return ap[q] if isinstance(q, int) else ap[bass.ds(q, 1)].rearrange("o p t d -> (o p) t d")

        uses = {MA: {"inputs": [(e_xTs, "group", 0)],
                     "V": [(e_V32, "group", 0), (e_gate, "group", 0)] if ret else [(e_Vl, "group", 0)],
                     "maxima": [] if ret else [(e_Qm, "tile", -2)],
                     "result": [(e_OTs, "group", -3)],
                     "K0": [(e_Ks[0], "group", 0)]},
                MB: {"QK": [(e_lo, "group", 0)],
                     "Q0": [(e_Qs[0], "group", 0)],
                     "out": [(e_r, "group", -3)],
                     "maxima": [] if ret else [(e_Qm, "tile", -1)]}}

        def bank_free(which, use, m, k, steps):
            names = [n_ for n_ in uses[which] if uses[which][n_]]
            i = names.index(use)
            for back in range(1, len(names) + 1):
                c = k // TPG - (1 if back > i else 0)
                found = False
                for ev, of, lag in uses[which][names[i - back]]:
                    j = c + lag if of == "group" else TPG * c + lag
                    per, total = (GPB, NQ) if of == "group" else (TPB, NT)
                    if steps is None or 0 <= m * per + j < total:
                        ev.wait(pe, (m, j))
                        found = True
                if found:
                    return

        def load(q):
            p = q[1] % 2
            y_before = (q[0], q[1] - 2)
            e_xb.wait(sp, (q[0], q[1] - 4))
            e_xT.wait(sp, (q[0], q[1] - 4))
            ld.mark(sp.dma_start(xg[q[1] % 4][:, :, :], dram(src_g, q)), q)
            if cross:
                e_xT.wait(sp, y_before)
                ldc.mark(sp.dma_start(cg[p][:, :, :], dram(ctx_g, q)), q)

        def turn_inputs(q, free):
            p = q[1] % 2
            free("inputs")
            ld.wait(pe, q)
            for t in range(TPG):
                i = pe.transpose(bankA[:, t * P:(t + 1) * P], xg[q[1] % 4][:, t, :], ident[:, :])
            if cross:
                ldc.wait(pe, q)
                for t in range(TPG):
                    i = pe.transpose(bankA[:, GT + t * P:GT + (t + 1) * P], cg[p][:, t, :], ident[:, :])
            e_xT.mark(i, q)
            e_V.wait(act, (q[0], q[1] - 2))
            e_xT.wait(act, q)
            n = 1 + kv
            e_xTs.mark(act.copy(srcT[p][:, 0:n, :].rearrange("p a t -> p (a t)"), bankA[:, 0:n * GT]), q)
            if causal:
                e_r.wait(act, (q[0], q[1] - 4))
                e_xb.mark(act.copy(xb[q[1] % 4][:, :, :].rearrange("p t d -> p (t d)"),
                                   xg[q[1] % 4][:, :, :].rearrange("p t d -> p (t d)")), q)
            else:
                e_r.wait(pool, (q[0], q[1] - 4))
                ld.wait(pool, q)
                e_xb.mark(pool.tensor_tensor(xb[q[1] % 4][:, :, :], xg[q[1] % 4][:, :, :],
                                               brow("a_bo" if ret else "x_bo"), ALU.add), q)

        def project_qk(q, free):
            p = q[1] % 2
            free("QK")
            e_xTs.wait(pe, q)
            pe.matmul(bankB[:, 0:GT], WQ, srcT[p][:, 0, :], start=True, stop=True)
            e_QK.mark(pe.matmul(bankB[:, GT:2 * GT], WK, srcT[p][:, kv, :], start=True, stop=True), q)
            e_sel[1].wait(act, (q[0], q[1] - 2))
            e_QK.wait(act, q)
            act.activation(hilo[p][:, 0, :], bankB[:, 0:GT], ACT.Identity, bias=column(bq))
            e_hi.mark(act.activation(hilo[p][:, 2, :], bankB[:, GT:2 * GT], ACT.Identity, bias=column(bk)), q)
            e_hi.wait(dve, q)
            dve.scalar_tensor_tensor(out=hilo[p][:, 1, :], in0=bankB[:, 0:GT], scalar=column(bq),
                                     in1=hilo[p][:, 0, :], op0=ALU.add, op1=ALU.subtract)
            e_lo.mark(dve.scalar_tensor_tensor(out=hilo[p][:, 3, :], in0=bankB[:, GT:2 * GT], scalar=column(bk),
                                                 in1=hilo[p][:, 2, :], op0=ALU.add, op1=ALU.subtract), q)

        def project_v(q, free):
            p = q[1] % 2
            free("V")
            for t in range(TPG):
                i = pe.matmul(bankA[:, t * P:(t + 1) * P], srcT[p][:, kv, t * P:(t + 1) * P], WV,
                              start=True, stop=True)
            if ret:
                i = pe.matmul(bankA[:, GT:2 * GT], W[:, w0 + 4, :], srcT[p][:, 0, :], start=True, stop=True)
            e_V.mark(i, q)

            def parts(v):
                return v.rearrange("p t (j e) -> p t j e", e=2 * DH)

            tiles_before = (q[0], TPG * (q[1] - 4) + TPG - 1)
            e_PV.wait(act, tiles_before)
            vh = Vh[q[1] % 4][:, :, :, 0:2 * DH]
            vp = bankA[:, 0:GT].rearrange("p (t j e) -> p t j e", t=TPG, e=2 * DH)
            if ret:
                e_V.wait(dve, q)
                e_V32.mark(dve.tensor_tensor(V32[p][:, :, :], bankA[:, 0:GT].rearrange("p (t d) -> p t d", t=TPG),
                                               brow("a_bv"), ALU.add), q)
                e_V32.wait(act, q)
                vp = V32[p][:, :, :].rearrange("p t (j e) -> p t j e", e=2 * DH)
                e_OTg.wait(act, (q[0], q[1] - 4))
                e_gate.mark(act.activation(GTs[q[1] % 4][:, :], bankA[:, GT:2 * GT], ACT.Sigmoid, bias=column("a_bg")), q)
            e_V.wait(act, q)
            for t in range(TPG):
                i = act.copy(vh[:, t], vp[:, t])
            e_Vh.mark(i, q)
            e_Vh.wait(dve, q)
            for t in range(TPG):
                i = dve.tensor_tensor(Vl[q[1] % 4][:, t], vp[:, t], vh[:, t], ALU.subtract)
            e_Vl.mark(i, q)

        def stack(q, j, free_q, free_k):
            p = q[1] % 2
            bank_q, bank_k = (bankB, bankA) if j == 0 else (bank[:, S_BANK, :], bank[:, S_BANK + 1, :])
            e_lo.wait(pe, q)
            free_q()
            for g in (2 * j, 2 * j + 1):
                o = bank_q[:, (g % 2) * GT:(g % 2 + 1) * GT]
                pe.matmul(o, sel[:, 0, g, :], hilo[p][:, 0, :], start=True, stop=False)
                pe.matmul(o, sel[:, 1, g, :], hilo[p][:, 1, :], start=False, stop=True)
            free_k()
            for g in (2 * j, 2 * j + 1):
                o = bank_k[:, (g % 2) * GT:(g % 2 + 1) * GT]
                pe.matmul(o, sel[:, 2, g, :], hilo[p][:, 2, :], start=True, stop=False)
                i = pe.matmul(o, sel[:, 3, g, :], hilo[p][:, 3, :], start=False, stop=True)
            e_sel[j].mark(i, q)
            tiles_before = (q[0], TPG * (q[1] - 2) + TPG - 1)
            for e in (act, dve):
                e_T.wait(e, tiles_before)
            e_sel[j].wait(act, q)
            e_Qs[j].mark(act.copy(Qst[p][:, 2 * j:2 * j + 2, :].rearrange("p g t -> p (g t)"), bank_q), q)
            e_sel[j].wait(dve, q)
            e_Ks[j].mark(dve.tensor_scalar(Kst[p][:, 2 * j:2 * j + 2, :].rearrange("p g t -> p (g t)"), bank_k,
                                             column("ones_row"), None, ALU.add), q)

        def group_of(n):
            return (n[0], n[1] // TPG)

        def score_tile(n, strips, banks, left, left_at, right, right_at):
            for i in range(4):
                if i >= 2:
                    strips[i - 2].wait(pe, n)
                for g in range(NG):
                    slot = 2 * g + i // 2
                    for b in range(2):
                        inst = pe.matmul(bank[64 * b:64 * b + 64, banks + i % 2, slot * S:(slot + 1) * S],
                                         left[32 * i:32 * i + 32, g, left_at + b * S:left_at + (b + 1) * S],
                                         right[32 * i:32 * i + 32, g, right_at + b * S:right_at + (b + 1) * S],
                                         start=True, stop=True)
                if i < 2:
                    strips[i].mark(inst, n)
            return inst

        def scores_s(n, stacked=None):
            if stacked is not None:
                e_Qs[1].wait(pe, stacked)
                e_Ks[1].wait(pe, stacked)
            q, p, t = group_of(n), group_of(n)[1] % 2, n[1] % 2
            if t == 0:
                e_Qs[1].wait(pe, q)
                e_Ks[1].wait(pe, q)
            (e_Sm if causal else e_mx).wait(pe, (n[0], n[1] - 1))
            at = (n[1] % TPG) * P
            e_S.mark(score_tile(n, e_Si, S_BANK, Qst[p], at, Kst[p], at), n)

        def maxima(n):
            scores = bank[:, S_BANK:S_BANK + 2, :].rearrange("p h (k s) -> p h k s", s=S)
            if causal:
                e_mx.wait(dve, (n[0], n[1] - 1))
                e_S.wait(dve, n)
                e_Sm.mark(dve.tensor_tensor(Sm[:, :, :], scores.rearrange("p h k s -> p (h k) s"),
                                            masks_f[:, 2 * S:].unsqueeze(1).broadcast_to([P, H, S]), ALU.add), n)
                scores = Sm[:, :, :].rearrange("p (h k) s -> p h k s", h=2)
                e_Sm.wait(dve, n)
            else:
                e_S.wait(dve, n)
            e_mT.wait(dve, (n[0], n[1] - 2))
            t = n[1] % 2
            full = mx[t][:, :, :].rearrange("p g (k h c) -> p h (g k) c", k=2, h=2, c=32)[:, :, :, MAX_ROW]
            e_mx.mark(dve.tensor_reduce(full, scores, AX_X, ALU.max, negate=True), n)

        def turn_maxima(n, free):
            t = n[1] % 2
            in_bank = bankB if t else bankA
            free("maxima")
            e_mx.wait(pe, n)
            for g in range(NG):
                i = pe.matmul(in_bank[:, g * P:(g + 1) * P], mx[t][:, g, :], ident16[:, :], start=True, stop=True)
            e_mT.mark(i, n)
            q = group_of(n)
            at = (n[1] % TPG) * P
            e_T.wait(dve, (n[0], n[1] - 2))
            e_mT.wait(dve, n)
            e_Qm.mark(dve.tensor_tensor(Qm[t][:, :, :], in_bank[:, :].rearrange("p (g s) -> p g s", g=NG),
                                          Qst[q[1] % 2][:, :, at:at + P], ALU.add), n)

        def scores_t(n):
            q, p, t = group_of(n), group_of(n)[1] % 2, n[1] % 2
            at = (n[1] % TPG) * P
            tb = (T_BANK if t else S_BANK) if ret else T_BANK
            if ret:
                if t == 0:
                    e_Qs[1].wait(pe, q)
                    e_Ks[1].wait(pe, q)
                e_P.wait(pe, (n[0], n[1] - 2))
                right, right_at = Qst[p], at
            else:
                e_Qm.wait(pe, n)
                (e_Tm if causal else e_P).wait(pe, (n[0], n[1] - 1))
                right, right_at = Qm[t], 0
            e_T.mark(score_tile(n, e_Ti, tb, Kst[p], at, right, right_at), n)

        def mask_weights(n):
            t = n[1] % 2
            e_P.wait(dve, (n[0], n[1] - 2))
            e_T.wait(dve, n)
            e_Tm.mark(dve.tensor_tensor(Tm[t][:, :, :], bank[:, T_BANK:T_BANK + 2, :].rearrange("p h (k s) -> p (h k) s", s=S),
                                        masks_f[:, S:2 * S].unsqueeze(1).broadcast_to([P, H, S]), ALU.add), n)

        def weights(n):
            t = n[1] % 2
            tb = (T_BANK if t else S_BANK) if ret else T_BANK
            e = dve if ret else act
            (e_Tm if causal else e_T).wait(e, n)
            e_PV.wait(e, (n[0], n[1] - 2))
            e_Pl.wait(e, (n[0], n[1] - 2))
            sc = Tm[t][:, :, :] if causal else bank[:, tb:tb + 2, :].rearrange("p h (k s) -> p (h k) s", s=S)
            if ret:
                e_P.mark(dve.tensor_tensor(P32[t][:, :, :], sc, decay.unsqueeze(1).broadcast_to([P, H, S]),
                                             ALU.mult), n)
            else:
                e_P.mark(act.activation(P32[t][:, :, :], sc, ACT.Exp, scale=SCALE), n)
            weights_lo(n)

        def upper(t):
            return P32[t][:, :, :].rearrange("p k s -> p (k s)").bitcast(BF16)[:, 1::2]

        def weights_lo(n):
            t = n[1] % 2
            e_P.wait(pool, n)
            e_PV.wait(pool, (n[0], n[1] - 2))
            e_Pl.mark(pool.tensor_tensor(Plo[t][:, :, :].rearrange("p k s -> p (k s)"),
                                           P32[t][:, :, :].rearrange("p k s -> p (k s)"), upper(t), ALU.subtract), n)

        def weighted_sums(n):
            q, p, t, tt = group_of(n), group_of(n)[1] % 2, n[1] % 2, n[1] % TPG
            nv = 2 * DH if ret else 2 * DH + 1
            e_Vl.wait(pe, q)
            e_O.wait(pe, (n[0], n[1] - 1))
            e_P.wait(pe, n)
            e_Pl.wait(pe, n)
            up = upper(t)
            lo = Plo[t][:, :, :].rearrange("p k s -> p (k s)")
            for b in range(2):
                rows_b = slice(64 * b, 64 * b + 64)
                for j in range(PAIRS):
                    c = slice(j * P, (j + 1) * P)
                    o = bank[:, PV_BANK + b, j * 32:j * 32 + nv]
                    pe.matmul(o, up[rows_b, c], Vh[q[1] % 4][rows_b, tt, j, 0:nv], start=True, stop=False)
                    pe.matmul(o, lo[rows_b, c], Vh[q[1] % 4][rows_b, tt, j, 0:nv], start=False, stop=False)
                    i = pe.matmul(o[:, 0:2 * DH], up[rows_b, c], Vl[q[1] % 4][rows_b, tt, j, :], start=False, stop=True)
            e_PV.mark(i, n)
            pv = bank[:, PV_BANK:PV_BANK + 2, 0:PAIRS * 32].rearrange("p b (j c) -> p b j c", c=32)
            e_OT.wait(dve, (q[0], q[1] - 2)) if not ret else e_On.wait(dve, (q[0], q[1] - 2))
            e_PV.wait(dve, n)
            if not ret:
                e_rd.mark(dve.reciprocal(rden[t][:, :, :], pv[:, :, :, 2 * DH]), n)
                e_rd.wait(dve, n)
            ov = O[p][:, tt, :].rearrange("p (j i e) -> p j i e", i=2, e=DH)
            for b in range(2):
                for i2 in range(2):
                    rs_ = slice(64 * i2, 64 * i2 + 64)
                    o = ov[64 * b:64 * b + 64, :, i2, :]
                    a = pv[rs_, b, :, i2 * DH:(i2 + 1) * DH]
                    if ret:
                        i = dve.tensor_copy(o, a)
                    else:
                        i = dve.tensor_tensor(o, a, rden[t][rs_, b, :].unsqueeze(2).broadcast_to([64, PAIRS, DH]),
                                              ALU.mult)
            e_O.mark(i, n)

        def norm_scalars(q, j, v, evs, ready):
            p = q[1] % 2
            s1, s2, s3, s4 = evs
            ready(dve)
            for t in range(TPG):
                i = dve.bn_stats(st[j][p][:, t, :], v[:, t, :])
            s1.mark(i, q)
            s1.wait(dve, q)
            carrier()
            for t in range(TPG):
                i = dve.bn_aggr(mv[j][p][:, t, :], st[j][p][:, t, :])
            s2.mark(i, q)
            s2.wait(dve, q)
            s3.mark(dve.tensor_scalar(ve[j][p][:, :, 0], mv[j][p][:, :, 1], EPS, None, ALU.add), q)
            s3.wait(pool, q)
            s4.mark(pool.tensor_tensor(rstd[j][p][:, :, 0], ve[j][p][:, :, 0], minus_half[:, :], ALU.pow), q)

        def normalise(q, j, o, v, rs, ev):
            p = q[1] % 2
            rs.wait(dve, q)
            for t in range(TPG):
                i = dve.tensor_scalar(o[:, t, :], v[:, t, :], mv[j][p][:, t, 0:1], rstd[j][p][:, t, :],
                                      ALU.subtract, ALU.mult)
            ev.mark(i, q)

        def retained_scalars(q):
            last = (q[0], TPG * q[1] + TPG - 1)
            norm_scalars(q, 0, O[q[1] % 2], (e_st, e_mv, e_ve, e_rs), lambda e: e_O.wait(e, last))

        def norm_retained(q):
            e_OT.wait(dve, (q[0], q[1] - 2))
            normalise(q, 0, On[q[1] % 2], O[q[1] % 2], e_rs, e_On)

        def turn_result(q, free):
            p = q[1] % 2
            free("result")
            if ret:
                e_On.wait(pe, q)
                v = On[p]
            else:
                e_O.wait(pe, (q[0], TPG * q[1] + TPG - 1))
                v = O[p]
            for t in range(TPG):
                i = pe.transpose(bankA[:, t * P:(t + 1) * P], v[:, t, :], ident[:, :])
            e_OT.mark(i, q)
            before = (q[0], q[1] - 2)
            if ret:
                e_OTg.wait(dve, before)
                e_OT.wait(dve, q)
                e_OTs.mark(dve.tensor_scalar(OT[p][:, :], bankA[:, 0:GT], column("a_gamma"), column("a_beta"),
                                               ALU.mult, ALU.add), q)
                e_OTs.wait(dve, q)
                e_gate.wait(dve, q)
                e_out.wait(dve, before)
                e_OTg.mark(dve.tensor_tensor(OTg[p][:, :], OT[p][:, :], GTs[q[1] % 4][:, :], ALU.mult), q)
            else:
                e_out.wait(act, before)
                e_OT.wait(act, q)
                e_OTs.mark(act.activation(OT[p][:, :], bankA[:, 0:GT], ACT.Identity,
                                            bias=column("x_bv" if cross else "k_zero")), q)

        def project_out(q, free):
            p = q[1] % 2
            src_t = OTg[p] if ret else OT[p]
            free("out")
            (e_OTg if ret else e_OTs).wait(pe, q)
            for t in range(TPG):
                i = pe.matmul(bankB[:, t * P:(t + 1) * P], src_t[:, t * P:(t + 1) * P], WO, start=True, stop=True)
            e_out.mark(i, q)
            e_out.wait(dve, q)
            e_xb.wait(dve, q)
            e_y.wait(dve, (q[0], q[1] - 2))
            e_r.mark(dve.tensor_tensor(r[p][:, :, :], bankB[:, 0:GT].rearrange("p (t d) -> p t d", t=TPG),
                                         xb[q[1] % 4][:, :, :], ALU.add), q)

        def result_scalars(q):
            norm_scalars(q, 1, r[q[1] % 2], (f_st, f_mv, f_ve, f_rs), lambda e: e_r.wait(e, q))

        def finish(q):
            p = q[1] % 2
            sto.wait(dve, (q[0], q[1] - 2))
            if not causal:
                normalise(q, 1, y[p], r[p], f_rs, e_y)
                return
            e_hn.wait(dve, (q[0], q[1] - 2))
            normalise(q, 1, hn[p], r[p], f_rs, e_hn)
            e_hn.wait(pool, q)
            e_hg.mark(pool.tensor_tensor(hg[p][:, :, :], hn[p][:, :, :], brow("g1"), ALU.mult), q)
            e_hg.wait(pool, q)
            sto.wait(pool, (q[0], q[1] - 2))
            e_y.mark(pool.tensor_tensor(y[p][:, :, :], hg[p][:, :, :], brow("b1"), ALU.add), q)

        def store(q):
            e_y.wait(act, q)
            sto.mark(act.dma_start(dram(dst_g, q), y[q[1] % 2][:, :, :]), q)

        def step(m, k, steps):

            def tile(lag):
                s = None if steps is None else steps - lag
                return (m, k - lag), s is None or 0 <= s < NT

            def group(lag):
                s = None if steps is None else (steps - lag) // TPG
                return (m, (k - lag) // TPG), s is None or 0 <= s < NQ

            def free_a(use):
                bank_free(MA, use, m, k, steps)

            def free_b(use):
                bank_free(MB, use, m, k, steps)

            q, on_q = group(k % 2)
            n_s, on_s = tile(2)
            n_t, on_t = tile(2 if ret else 3)
            n_w, on_w = tile(3 if ret else 4)
            q_o, on_o = group(6 + k % 2)
            if k % 2 == 0:
                q_f, on_f = group(8)
                if ret and k == TPB // 2 and (steps is None or steps < NT):
                    clear_blocks(m)
                if on_q:
                    load(q)
                    turn_inputs(q, free_a)
                if not ret and on_w:
                    weights(n_w)
                if not ret and on_s:
                    scores_s(n_s)
                    maxima(n_s)
                if not causal and on_f:
                    result_scalars(q_f)
                if ret and on_o:
                    norm_retained(q_o)
                if ret and on_t:
                    scores_t(n_t)
                    weights(n_t)
                if on_q:
                    project_qk(q, free_b)
                if on_q:
                    project_v(q, free_a)
                if on_w:
                    weighted_sums(n_w)
                if not ret and on_s:
                    turn_maxima(n_s, free_a)
                if causal and on_f:
                    result_scalars(q_f)
                if not ret and on_t:
                    scores_t(n_t)
                if causal and on_t:
                    mask_weights(n_t)
                if on_o:
                    turn_result(q_o, free_a)
                if not ret and on_t:
                    weights(n_t)
                if on_f:
                    finish(q_f)
            else:
                q_r, on_r = group(5)
                q_f, on_f = group(9)
                n_e, on_e = tile(3)
                if on_q:
                    def free_even():
                        if on_e:
                            (e_P if ret else e_Sm if causal else e_mx).wait(pe, n_e)

                    stack(q, 0, lambda: free_b("Q0"), lambda: free_a("K0"))
                    stack(q, 1, free_even, lambda: None)
                if on_o:
                    project_out(q_o, free_b)
                if on_t:
                    scores_t(n_t)
                if ret and on_t:
                    weights(n_t)
                if ret and on_r:
                    retained_scalars(q_r)
                if not ret and on_s:
                    scores_s(n_s, q if on_q else None)
                    maxima(n_s)
                if causal and on_t:
                    mask_weights(n_t)
                if on_w:
                    weighted_sums(n_w)
                if not ret and on_s:
                    turn_maxima(n_s, free_b)
                if on_f:
                    store(q_f)

        for k in range(TPB):
            step(0, k, k)
        if ret:
            load_mixture()
        with nc.Fori(1, NB) as m:
            for k in range(TPB):
                step(m, k, None)
        for k in range(TPB):
            step(NB, k, NB * TPB + k)
        for k in (GPB - 2, GPB - 1):
            sto.wait(sp, (NB - 1, k))
        barrier()
        for e in events:
            if e not in unused:
                e.happened(NB)


    def moe_phase(h_src, x_src, dst):
        attention_ctx.close()
        free.extend(events)
        events.clear()
        h_t = [sb(f"h_t{p}", [P, MT, P]) for p in range(2)]
        x_t = [sb(f"x_t{p}", [P, MT, P]) for p in range(2)]
        ya_t = [sb(f"ya_t{p}", [P, MT, P]) for p in range(2)]
        yb_t = [sb(f"yb_t{p}", [P, MT, P]) for p in range(2)]
        hT = [sb(f"hT{p}", [P, MT * P]) for p in range(2)]
        lg = sb("lg", [P, NT, E_N])
        lg2 = sb("lg2", [P, NT, E_N])
        eq = sb("eq", [P, NT, E_N])
        pr = sb("pr", [P, NT, E_N])
        m12 = sb("m12", [P, 2, NT])
        r12 = sb("r12", [P, 2, NT])
        oh = sb("oh", [P, E_N, 2, NT])
        spread = sb("spread", [P, E_N, U])
        slot2 = sb("slot2", [P, E_N, U])
        tot = sb("tot", [P, E_N])
        cmp_ = sb("cmp_", [P, E_N, NT])
        cmpb = sb("cmpb", [P, NBLK, E_N - 1])
        nb = sb("nb", [P, E_N])
        pre = [sb(f"pre{j}", [P, 2 * E_N]) for j in range(4)]
        start = sb("start", [P, E_N])
        slotf = sb("slotf", [P, U])
        slots = sb("slots", [P, U], U32)
        ebf = sb("ebf", [P, NBLK])
        expert_of = sb("expert_of", [P, NBLK], mybir.dt.int32)
        d12 = sb("d12", [P, NT])
        e12 = sb("e12", [P, NT])
        s12 = sb("s12", [P, NT])
        wa = sb("wa", [P, NT])
        wb = sb("wb", [P, NT])
        hx = [sb(f"hx{p}", [P, 2, RW]) for p in range(4)]
        ix = [sb(f"ix{p}", [P, 2], U32) for p in range(4)]
        xrow = [sb(f"xrow{p}", [P, RW]) for p in range(4)]
        ix2 = [sb(f"ix2_{p}", [P, 1], U32) for p in range(4)]
        hTb = [sb(f"hTb{p}", [P, P]) for p in range(2)]
        we = [sb(f"we{p}", [P, WW]) for p in range(4)]
        G = [sb(f"G{p}", [P, FC, P]) for p in range(4)]
        yo = [sb(f"yo{p}", [P, P]) for p in range(2)]
        acc = [sb(f"acc{p}", [P, MT, P]) for p in range(2)]
        t2a = [sb(f"t2a_{p}", [P, MT, P]) for p in range(2)]
        t1 = [sb(f"t1_{p}", [P, MT, P]) for p in range(2)]
        t2 = [sb(f"t2_{p}", [P, MT, P]) for p in range(2)]
        t3 = [sb(f"t3_{p}", [P, MT, P]) for p in range(2)]
        res = [sb(f"res{p}", [P, MT, P]) for p in range(2)]
        mst = [sb(f"mst{p}", [P, MT, 6]) for p in range(4)]
        mmv = [sb(f"mmv{p}", [P, MT, 2]) for p in range(4)]
        mve = [sb(f"mve{p}", [P, MT]) for p in range(4)]
        mrs = [sb(f"mrs{p}", [P, MT]) for p in range(4)]
        nmean = [sb(f"nmean{p}", [P, MT]) for p in range(4)]
        nmr = [sb(f"nmr{p}", [P, MT]) for p in range(4)]
        mh4 = sb("mh4", [P, MT])
        by_tile = h_src.rearrange("(t p) d -> t p d", p=P)
        by_block = buf.rearrange("(b p) w -> b p w", p=P)

        def item(ap, i):
            if isinstance(i, int):
                return ap[i]
            letters = " ".join("abcd"[:len(ap.shape) - 2])
            return ap[bass.ds(i, 1)].rearrange(f"o p {letters} -> (o p) {letters}")

        def at(idx, per):
            return idx[0] * per + idx[1]

        def columns(i, n):
            return slice(i, i + n) if isinstance(i, int) else bass.ds(i, n)

        def pool_carrier():
            carriers[1] += 1
            return pool.tensor_tensor(junk_p[:, carriers[1]:carriers[1] + 1], minus_half[:, 0:1], minus_half[:, 0:1], ALU.add)

        def pipeline(per, bodies, depth, step):
            for k in range(per):
                step(0, k, k)
            with nc.Fori(1, bodies) as m:
                for k in range(per):
                    step(m, k, None)
            for k in range(depth):
                step(bodies, k, bodies * per + k)

        def over(bodies):
            barrier()
            for e_ in events:
                e_.happened(bodies)
            free.extend(e_ for e_ in events if not e_.fresh)
            events.clear()

        def lagged(m, k, steps, lag, total):
            s = None if steps is None else steps - lag
            return (m, k - lag), s is None or 0 <= s < total

        r_ld = event("r_ld", 2, 16)
        r_hT, r_hTs, r_lg, r_lgs = (event(n, 2) for n in ("r_hT", "r_hTs", "r_lg", "r_lgs"))
        h_by_step = h_src.rearrange("(q t p) d -> q p t d", t=MT, p=P)
        x_by_step = x_src.rearrange("(q t p) d -> q p t d", t=MT, p=P)
        o_by_step = dst.rearrange("(q t p) d -> q p t d", t=MT, p=P)

        pool.memset(mh4[:, :], -0.5).then_inc(s_set, 1)
        pool.memset(ones[:, :], 1.0).then_inc(s_set, 1)
        pool.memset(pre[0][:, 0:E_N], 0.0).then_inc(s_set, 1)
        pool.memset(pre[1][:, 0:E_N], 0.0).then_inc(s_set, 1)
        pool.memset(pre[2][:, 0:E_N], 0.0).then_inc(s_set, 1)
        for e in (pe, dve, act, pool):
            e.wait_ge(s_w, moe_loads)
            e.wait_ge(s_set, 14)

        def router(m, k, steps):
            s0, on0 = lagged(m, k, steps, 0, NS)
            s1, on1 = lagged(m, k, steps, 1, NS)
            if on0:
                p = s0[1] % 2
                before = (s0[0], s0[1] - 2)
                r_hT.wait(sp, before)
                r_ld.mark(sp.dma_start(h_t[p][:, :, :], item(h_by_step, at(s0, 2))), s0)
                r_ld.wait(pe, s0)
                r_hTs.wait(pe, before)
                for t in range(MT):
                    i = pe.transpose(bank[:, p, t * P:(t + 1) * P], h_t[p][:, t, :], ident[:, :])
                r_hT.mark(i, s0)
                r_lg.wait(act, before)
                r_hT.wait(act, s0)
                r_hTs.mark(act.copy(hT[p][:, :], bank[:, p, :]), s0)
            if on1:
                p = s1[1] % 2
                r_hTs.wait(pe, s1)
                r_lgs.wait(pe, (s1[0], s1[1] - 2))
                for t in range(MT):
                    i = pe.matmul(bank[:, 2 + p, t * E_N:(t + 1) * E_N], hT[p][:, t * P:(t + 1) * P], wg_sb[:, :],
                                  start=True, stop=True)
                r_lg.mark(i, s1)
                r_lgs.wait(dve, (s1[0], s1[1] - 2))
                r_lg.wait(dve, s1)
                carrier()
                r_lgs.mark(dve.tensor_copy(lg[:, columns(at(s1, 2) * MT, MT), :],
                                           bank[:, 2 + p, 0:MT * E_N].rearrange("p (t e) -> p t e", e=E_N)), s1)

        pipeline(2, NS // 2, 1, router)
        for k in range(2):
            r_lgs.wait(dve, (NS // 2 - 1, k))
        over(NS // 2)

        s_dve = ctx.enter_context(nc.semaphore("s_dve"))
        s_pe = ctx.enter_context(nc.semaphore("s_pe"))
        s_act = ctx.enter_context(nc.semaphore("s_act"))
        n = [0]

        def chain(inst):
            n[0] += 1
            inst.then_inc(s_dve, 1)
            dve.wait_ge(s_dve, n[0])

        rev_b = rev[:, :].unsqueeze(1).broadcast_to([P, NT, E_N])
        for c, src_l in ((0, lg), (1, lg2)):
            ohv = oh[:, :, c, :].rearrange("p e t -> p t e")
            chain(dve.tensor_reduce(m12[:, c, :], src_l[:, :, :], AX_X, ALU.max))
            chain(dve.tensor_tensor(eq[:, :, :], src_l[:, :, :], m12[:, c, :].unsqueeze(2).broadcast_to([P, NT, E_N]),
                                    ALU.is_equal))
            chain(dve.tensor_tensor(pr[:, :, :], eq[:, :, :], rev_b, ALU.mult))
            chain(dve.tensor_reduce(r12[:, c, :], pr[:, :, :], AX_X, ALU.max))
            chain(dve.tensor_tensor(ohv, rev_b, r12[:, c, :].unsqueeze(2).broadcast_to([P, NT, E_N]), ALU.is_equal))
            if c == 0:
                chain(dve.scalar_tensor_tensor(out=lg2[:, :, :], in0=ohv, scalar=-1e30, in1=lg[:, :, :],
                                               op0=ALU.mult, op1=ALU.add))
        pe.wait_ge(s_dve, n[0])
        for e in range(E_N):
            i = pe.matmul(bank[0:U, 0, e:e + 1], oh[:, e, :, :].rearrange("p c t -> p (c t)"), ones[:, 0:1],
                          start=True, stop=True)
        i.then_inc(s_pe, 1)
        chain(dve.tensor_tensor(d12[:, :], m12[:, 1, :], m12[:, 0, :], ALU.subtract))
        act.wait_ge(s_dve, n[0])
        act.activation(e12[:, :], d12[:, :], ACT.Exp).then_inc(s_act, 1)
        dve.wait_ge(s_pe, 1)
        chain(dve.tensor_copy(tot[0:U, :], bank[0:U, 0, 0:E_N]))
        chain(dve.tensor_tensor(spread[0:U, :, :], tri[0:U, 0:U].unsqueeze(1).broadcast_to([U, E_N, U]),
                                tot[0:U, :].unsqueeze(2).broadcast_to([U, E_N, U]), ALU.mult))
        pe.wait_ge(s_dve, n[0])
        pe.matmul(bank[:, 1, 0:E_N], ones[0:U, :], tot[0:U, :], start=True, stop=True).then_inc(s_pe, 1)
        ohf = oh[:, :, :, :].rearrange("p e c t -> p (e c t)")
        spf = spread[:, :, :].rearrange("p e u -> p (e u)")
        half = E_N * U // 2
        for h in range(2):
            o = bank[:, 2 + h, 0:half]
            pe.matmul(o, tri[:, :], ohf[:, h * half:(h + 1) * half], start=True, stop=False)
            i = pe.matmul(o, ones[0:U, :], spf[0:U, h * half:(h + 1) * half], start=False, stop=True)
        i.then_inc(s_pe, 1)
        dve.wait_ge(s_pe, 2)
        chain(dve.tensor_tensor(cmp_[:, :, :], bank[:, 1, 0:E_N].unsqueeze(2).broadcast_to([P, E_N, NT]),
                                steps128[:, :].unsqueeze(1).broadcast_to([P, E_N, NT]), ALU.is_gt))
        chain(dve.tensor_reduce(pre[0][:, E_N:], cmp_[:, :, :], AX_X, ALU.add))
        for j in range(3):
            chain(dve.tensor_tensor(pre[j + 1][:, E_N:], pre[j][:, E_N:], pre[j][:, E_N - 2 ** j:2 * E_N - 2 ** j], ALU.add))
        last = pre[3][:, E_N:]
        chain(dve.tensor_tensor(nb[:, :], last, pre[0][:, E_N:], ALU.subtract))
        chain(dve.tensor_scalar(start[:, :], nb[:, :], float(P), None, ALU.mult))
        dve.wait_ge(s_pe, 3)
        for h in range(2):
            es = slice(h * E_N // 2, (h + 1) * E_N // 2)
            i = dve.tensor_tensor(slot2[:, es, :], bank[:, 2 + h, 0:half].rearrange("p (e u) -> p e u", u=U),
                                  start[:, es].unsqueeze(2).broadcast_to([P, E_N // 2, U]), ALU.add)
        chain(i)
        chain(dve.tensor_tensor(spread[:, :, :], slot2[:, :, :], oh[:, :, :, :].rearrange("p e c t -> p e (c t)"), ALU.mult))
        chain(dve.tensor_reduce(slotf[:, :], spread[:, :, :].rearrange("p e u -> p u e"), AX_X, ALU.add))
        chain(dve.tensor_copy(slots[:, :], slotf[:, :]))
        chain(dve.tensor_tensor(cmpb[:, :, :], last[:, 0:E_N - 1].unsqueeze(1).broadcast_to([P, NBLK, E_N - 1]),
                                blocks_row[:, :].unsqueeze(2).broadcast_to([P, NBLK, E_N - 1]), ALU.is_le))
        chain(dve.tensor_reduce(ebf[:, :], cmpb[:, :, :], AX_X, ALU.add))
        chain(dve.tensor_copy(expert_of[:, :], ebf[:, :]))
        dve.wait_ge(s_act, 1)
        chain(dve.tensor_scalar(s12[:, :], e12[:, :], 1.0, None, ALU.add))
        chain(dve.reciprocal(wa[:, :], s12[:, :]))
        chain(dve.tensor_tensor(wb[:, :], wa[:, :], e12[:, :], ALU.mult))

        d_ld = event("d_ld", BPB, 32, 4)
        d_ix = event("d_ix", BPB, 1, 4)
        d_sc = event("d_sc", BPB, 32, 4, fresh=True)
        pool.wait_ge(s_fill, 16 * NB)

        d_go = event("d_go", BPB, 1, 4)

        def dispatch(m, k, steps):
            t, on = lagged(m, k, steps, 0, NT)
            b = k % 4
            before = (t[0], t[1] - 4)
            d_sc.wait(sp, before)
            for c in range(2):
                sp.dma_start(hx[b][:, c, 0:P], item(by_tile, at(t, BPB))).then_inc(d_ld.at(t)[0], 16)
            d_sc.wait(dve, before)
            carrier()
            dve.tensor_copy(hx[b][:, :, P], ids[:, :, columns(at(t, BPB), 1)].rearrange("p c t -> p (c t)"))
            sl = slots[:, :].rearrange("p (c t) -> p c t", c=2)
            d_ix.mark(dve.tensor_copy(ix[b][:, :], sl[:, :, columns(at(t, BPB), 1)].rearrange("p c t -> p (c t)")), t)
            d_go.wait(pool, before)
            d_ld.wait(pool, t)
            pool_carrier()
            d_ix.wait(pool, t)
            d_go.mark(pool_carrier(), t)
            for c in range(2):
                pool.indirect_dma_start(buf[:, :], bass.IndirectOffsetOnAxis(ix[b][:, c:c + 1], 0), hx[b][:, c, :],
                                        None).then_inc(d_sc.at(t)[0], 16)

        pipeline(BPB, NT // BPB, 0, dispatch)
        for k in range(4):
            d_sc.wait(sp, (NT // BPB - 1, k))
        over(NT // BPB)

        b_ld = event("b_ld", EPB, 16, 4)
        b_xT, b_xTs, b_we, b_z, b_g, b_y, b_ix, b_yo = (event(n_, EPB) for n_ in
                                                  ("b_xT", "b_xTs", "b_we", "b_z", "b_g", "b_y", "b_ix", "b_yo"))
        b_sc = event("b_sc", EPB, 16, fresh=True)
        b_go = event("b_go", EPB)

        def expert(m, k, steps):
            s0, on0 = lagged(m, k, steps, 0, NBLK)
            s1, on1 = lagged(m, k, steps, 1, NBLK)
            s3, on3 = lagged(m, k, steps, 3, NBLK)
            if on3:
                p, b = s3[1] % 2, s3[1] % 4
                before = (s3[0], s3[1] - 2)
                b_g.wait(pe, s3)
                b_yo.wait(pe, before)
                for c in range(FC):
                    i = pe.matmul(bank[:, 4 + p, 0:P], G[b][:, c, :], we[b][:, W2 + c * P:W2 + (c + 1) * P],
                                  start=c == 0, stop=c == FC - 1)
                b_y.mark(i, s3)
                b_sc.wait(dve, before)
                b_y.wait(dve, s3)
                b_yo.mark(dve.tensor_tensor(yo[p][:, :], bank[:, 4 + p, 0:P], we[b][:, B2:B2 + P], ALU.add), s3)
                b_go.wait(pool, before)
                b_ix.wait(pool, s3)
                pool_carrier()
                b_yo.wait(pool, s3)
                b_go.mark(pool_carrier(), s3)
                b_sc.mark(pool.indirect_dma_start(ydst[:, :], bass.IndirectOffsetOnAxis(ix2[b][:, :], 0), yo[p][:, :],
                                                  None), s3)
            if on0:
                p, b = s0[1] % 2, s0[1] % 4
                before = (s0[0], s0[1] - 4)
                b_xT.wait(sp, before)
                b_ix.wait(sp, before)
                b_ld.mark(sp.dma_start(xrow[b][:, :], item(by_block, at(s0, EPB))), s0)
                b_ld.wait(pe, s0)
                b_xTs.wait(pe, (s0[0], s0[1] - 2))
                b_xT.mark(pe.transpose(bank[:, p, 0:P], xrow[b][:, 0:P], ident[:, :]), s0)
                b_z.wait(act, (s0[0], s0[1] - 2))
                b_xT.wait(act, s0)
                b_xTs.mark(act.copy(hTb[p][:, :], bank[:, p, 0:P]), s0)
                e = dve.value_load(expert_of[0:1, columns(at(s0, EPB), 1)], min_val=0, max_val=E_N - 1)
                b_y.wait(dve, before)
                b_g.wait(dve, before)
                b_yo.wait(dve, before)
                carrier()
                b_we.mark(dve.tensor_copy(we[b][:, :], wx[:, bass.ds(e, 1), :].rearrange("p o w -> p (o w)")), s0)
                b_ld.wait(pool, s0)
                b_sc.wait(pool, before)
                pool_carrier()
                b_ix.mark(pool.tensor_scalar(ix2[b][:, :], xrow[b][:, P:P + 1], trash[:, p:p + 1], None, ALU.max), s0)
            if on1:
                p, b = s1[1] % 2, s1[1] % 4
                before = (s1[0], s1[1] - 2)
                b_xTs.wait(pe, s1)
                b_we.wait(pe, s1)
                b_g.wait(pe, before)
                for c in range(FC):
                    i = pe.matmul(bank[:, 2 + p, c * P:(c + 1) * P], we[b][:, W1 + c * P:W1 + (c + 1) * P],
                                  hTb[p][:, :], start=True, stop=True)
                b_z.mark(i, s1)
                b_y.wait(act, (s1[0], s1[1] - 4))
                b_we.wait(act, s1)
                b_z.wait(act, s1)
                for c in range(FC):
                    i = act.activation(G[b][:, c, :], bank[:, 2 + p, c * P:(c + 1) * P], ACT.Gelu_apprx_tanh,
                                       bias=we[b][:, B1 + c:B1 + c + 1])
                b_g.mark(i, s1)

        pipeline(EPB, NBLK // EPB, 3, expert)
        for k in range(2):
            b_sc.wait(sp, (NBLK // EPB - 1, EPB - 2 + k))
        over(NBLK // EPB)

        CPB = 4
        f_st_ = event("g_sto", CPB, 16)
        f_ld = event("f_ld", CPB, 48)
        f_x = event("f_x", CPB, 16)
        f_half, f_acc = (event(n_, CPB) for n_ in ("g_half", "g_acc"))
        f_t1 = event("g_t1", CPB)
        f_t2a, f_t2 = (event(n_, CPB) for n_ in ("g_t2a", "g_t2"))
        f_t3 = event("g_t3", CPB)
        f_res = event("g_res", CPB)
        norms = [[event(f"g_{w_}{j}", CPB) for w_ in ("st", "mv", "ve", "rs")] for j in range(2)]
        g_pw = [event(f"g_pw{j}", CPB) for j in range(2)]
        y_by_step = [ydst[TRASH + c * T_N:TRASH + (c + 1) * T_N, :].rearrange("(q t p) d -> q p t d", t=MT, p=P)
                     for c in range(2)]

        def scalars(norms_now):
            for j, s, v, ready in norms_now:
                w = 2 * j + s[1] % 2
                ready.wait(dve, s)
                carrier()
                for t in range(MT):
                    i = dve.bn_stats(mst[w][:, t, :], v[:, t, :])
                norms[j][0].mark(i, s)
            for j, s, v, ready in norms_now:
                w = 2 * j + s[1] % 2
                norms[j][0].wait(dve, s)
                carrier()
                for t in range(MT):
                    i = dve.bn_aggr(mmv[w][:, t, :], mst[w][:, t, :])
                norms[j][1].mark(i, s)
            for j, s, v, ready in norms_now:
                w = 2 * j + s[1] % 2
                before = (s[0], s[1] - 2)
                norms[j][3].wait(dve, before)
                norms[j][1].wait(dve, s)
                dve.tensor_scalar(mve[w][:, :], mmv[w][:, :, 1], EPS, None, ALU.add)
                norms[j][2].mark(dve.tensor_scalar(nmean[w][:, :], mmv[w][:, :, 0], -1.0, None, ALU.mult), s)
                (f_t1, f_res)[j].wait(pool, before)
                norms[j][2].wait(pool, s)
                g_pw[j].mark(pool.tensor_tensor(mrs[w][:, :], mve[w][:, :], mh4[:, :], ALU.pow), s)
                g_pw[j].wait(pool, s)
                norms[j][3].mark(pool.tensor_tensor(nmr[w][:, :], nmean[w][:, :], mrs[w][:, :], ALU.mult), s)

        def normed(j, s, o, v):
            w = 2 * j + s[1] % 2
            norms[j][3].wait(act, s)
            for t in range(MT):
                i = act.activation(o[:, t, :], v[:, t, :], ACT.Identity, bias=nmr[w][:, t:t + 1], scale=mrs[w][:, t:t + 1])
            return i

        def br(name):
            return row[:, ROWS.index(name), :].unsqueeze(1).broadcast_to([P, MT, P])

        def combine(m, k, steps):
            s0, on0 = lagged(m, k, steps, 0, NS)
            s1, on1 = lagged(m, k, steps, 1, NS)
            s2, on2 = lagged(m, k, steps, 2, NS)
            s3, on3 = lagged(m, k, steps, 3, NS)
            now = []
            if on0:
                p = s0[1] % 2
                before = (s0[0], s0[1] - 2)
                f_acc.wait(sp, before)
                at0 = at(s0, CPB)
                for d_, s_ in ((h_t, h_by_step), (ya_t, y_by_step[0]), (yb_t, y_by_step[1])):
                    sp.dma_start(d_[p][:, :, :], item(s_, at0)).then_inc(f_ld.at(s0)[0], 16)
                f_t1.wait(dve, before)
                f_ld.wait(dve, s0)
                carrier()
                at0 = at0 * MT
                for t in range(MT):
                    i = dve.scalar_tensor_tensor(out=acc[p][:, t, :], in0=ya_t[p][:, t, :], scalar=wa[:, columns(at0 + t, 1)],
                                                 in1=h_t[p][:, t, :], op0=ALU.mult, op1=ALU.add)
                f_half.mark(i, s0)
                f_half.wait(dve, s0)
                for t in range(MT):
                    i = dve.scalar_tensor_tensor(out=acc[p][:, t, :], in0=yb_t[p][:, t, :], scalar=wb[:, columns(at0 + t, 1)],
                                                 in1=acc[p][:, t, :], op0=ALU.mult, op1=ALU.add)
                f_acc.mark(i, s0)
                now.append((0, s0, acc[p], f_acc))
            if on1:
                p = s1[1] % 2
                before = (s1[0], s1[1] - 2)
                f_t3.wait(sp, before)
                f_x.mark(sp.dma_start(x_t[p][:, :, :], item(x_by_step, at(s1, CPB))), s1)
                f_t2a.wait(act, before)
                f_t1.mark(normed(0, s1, t1[p], acc[p]), s1)
                f_t1.wait(pool, s1)
                f_t2a.mark(pool.tensor_tensor(t2a[p][:, :, :], t1[p][:, :, :], br("g2"), ALU.mult), s1)
                f_t3.wait(pool, before)
                f_t2a.wait(pool, s1)
                f_t2.mark(pool.tensor_tensor(t2[p][:, :, :], t2a[p][:, :, :], br("b2"), ALU.add), s1)
            if on2:
                p = s2[1] % 2
                f_x.wait(dve, s2)
                f_t2.wait(dve, s2)
                f_res.wait(dve, (s2[0], s2[1] - 2))
                f_t3.mark(dve.tensor_tensor(t3[p][:, :, :], t2[p][:, :, :], x_t[p][:, :, :], ALU.add), s2)
                now.append((1, s2, t3[p], f_t3))
            scalars(now)
            if on3:
                p = s3[1] % 2
                f_st_.wait(act, (s3[0], s3[1] - 2))
                f_res.mark(normed(1, s3, res[p], t3[p]), s3)
                f_res.wait(act, s3)
                f_st_.mark(act.dma_start(item(o_by_step, at(s3, CPB)), res[p][:, :, :]), s3)

        pipeline(CPB, NS // CPB, 3, combine)
        for k in (CPB - 2, CPB - 1):
            f_st_.wait(sp, (NS // CPB - 1, k))

    xf = x.rearrange("b s d -> (b s) d")
    ctxt = ctxt.rearrange("b s d -> (b s) d")
    outf = out.rearrange("b s d -> (b s) d")
    targets = [x1, x2, hd]
    softmax_only = [e_S, *e_Si, e_mx, e_mT, e_Qm, e_rd]
    self_only = [e_hn, e_hg, e_Sm, e_Tm]
    retention_only = [e_V32, e_gate, e_OTg, e_st, e_mv, e_ve, e_rs, e_On]
    attention_phase("ret", xf, outf if upto == 1 else x1, [ldc, *softmax_only, *self_only])
    if upto >= 2:
        attention_phase("cross", x1, outf if upto == 2 else x2, [*retention_only, *self_only])
    if upto >= 3:
        attention_phase("self", x2, outf if upto == 3 else hd, [ldc, *retention_only])
    if upto >= 4:
        moe_phase(hd, x2, outf)
    return ctx, events


def lay_out(inputs):
    a = {k: np.asarray(v) for k, v in inputs.items()}
    A, X, N = (lambda n: a["L0_attn_" + n]), (lambda n: a["L0_xattn_" + n]), (lambda n: a["L0_ffn_" + n])
    ident, sel, masks, ones_row = shape_constants()
    qkv = N("w_qkv")
    wmats = np.stack([A("Wq"), A("Wk"), A("Wv"), A("Wo"), A("Wg"),
                      X("wq_w").T, X("wk_w").T, X("wv_w").T, X("wo_w").T,
                      qkv[:, 0:P], qkv[:, P:2 * P], qkv[:, 2 * P:], N("w_o")])
    cols = np.stack([A("bq"), A("bk"), A("bg"), A("gamma"), A("beta"), X("wq_b"), X("wk_b"), X("wv_b"),
                     ones_row, np.zeros(P, np.float32)], 1)
    rows = np.stack([A("bv"), A("bo"), X("wo_b"), N("g1"), N("b1"), N("g2"), N("b2")])
    c = np.ascontiguousarray
    return {"x": a["x"], "ctxt": a["ctx_1024"], "wmats": c(wmats), "cols": c(cols), "rows": c(rows),
            "const_ident": ident, "const_sel": sel, "const_masks": masks, **routing_constants(a["x"].shape[0] * S // P), "wg": N("wg"),
            "w1": N("w1"), "bb1t": c(N("bb1").reshape(E_N * FC, P).T), "w2": N("w2"), "bb2": N("bb2")}


def kernel(**inputs):
    import concourse.bacc as _bacc
    from concourse.bass_utils import run_bass_kernel_spmd as _run

    nc = _bacc.Bacc("TRN2", target_bir_lowering=False, num_devices=1)
    arrays = lay_out(inputs)
    args = {n: nc.dram_tensor(n, a.shape, mybir.dt.from_np(a.dtype), kind="ExternalInput").ap()
            for n, a in arrays.items()}
    out = nc.dram_tensor("out", arrays["x"].shape, F32, kind="ExternalOutput").ap()
    build(nc, **args, out=out)
    r = _run(nc, [arrays], core_ids=[0])
    return r.results[0]["out"]
```
